# Optimizing a Trainium2 kernel written in Bass

```python
import numpy as np
import jax
import jax.numpy as jnp

def _softmax(x, axis=-1):
    return jax.nn.softmax(x, axis=axis)

def _gelu(x):
    return jax.nn.gelu(x, approximate=True)

def _silu(x):
    return jax.nn.silu(x)

def _sigmoid(x):
    return jax.nn.sigmoid(x)

def _layernorm(x, axis=-1, eps=1e-05):
    m = jnp.mean(x, axis=axis, keepdims=True)
    v = jnp.var(x, axis=axis, keepdims=True)
    return (x - m) / jnp.sqrt(v + eps)

def _scatter_add(tgt, idx, src, axis=0):
    return tgt.at[idx].add(src)

def _segment_sum(src, seg, n):
    return jax.ops.segment_sum(src, seg, n)
kernel_name = 'mk_adaln_ffn_d2_seqx_r8_c5d1bc'

def setup_inputs(seed: int=0):
    np.random.seed(seed)
    _w = jnp.asarray

    def _rec_inputs():
        import jax
        import jax.numpy as jnp
        _rk = jax.random.key(seed)
        x = -0.000125 + 0.9999 * jax.random.normal(jax.random.fold_in(_rk, 1), (64, 32, 512), jnp.float32)
        _lenS = 32 - jax.random.randint(jax.random.fold_in(_rk, 7), (64,), 0, max(1, 32 // 4) + 1, jnp.int32)
        _lenS2 = 32 - jax.random.randint(jax.random.fold_in(_rk, 8), (64,), 0, max(1, 32 // 4) + 1, jnp.int32)
        cond_128 = 0.0061147 + 1.02565 * jax.random.normal(jax.random.fold_in(_rk, 11), (64, 128), jnp.float32)
        fside_S_0 = -0.022604 + 0.987366 * jax.random.normal(jax.random.fold_in(_rk, 12), (32,), jnp.float32)
        return (x, cond_128, fside_S_0)
    x, cond_128, fside_S_0 = _rec_inputs()

    def _L0_cond_setup():
        import jax, jax.numpy as jnp
        import numpy as np
        K = 8
        T = 1.0
        D_EMBD = 128
        IN_C = 32
        OUT_C = 32
        BS = 32
        H = 512
        HID = 128
        key = jax.random.key(seed)
        ks = jax.random.split(key, 10)
        s = lambda fan_in: 1.0 / np.sqrt(fan_in)
        return {'x': jax.random.normal(ks[0], (BS, IN_C, H), dtype=jnp.float32), 'embedding': jax.random.normal(ks[1], (BS, D_EMBD), dtype=jnp.float32), 'W0': jax.random.normal(ks[2], (D_EMBD, HID), dtype=jnp.float32) * s(D_EMBD), 'b0': jnp.zeros((HID,), dtype=jnp.float32), 'W1': jax.random.normal(ks[3], (HID, HID), dtype=jnp.float32) * s(HID), 'b1': jnp.zeros((HID,), dtype=jnp.float32), 'W2': jax.random.normal(ks[4], (HID, K), dtype=jnp.float32) * s(HID), 'b2': jnp.zeros((K,), dtype=jnp.float32), 'weight': jax.random.normal(ks[5], (K, OUT_C, IN_C, 1), dtype=jnp.float32) * s(IN_C), 'bias_k': jax.random.normal(ks[6], (K, OUT_C), dtype=jnp.float32) * 0.1}
    _L0_cond_all = _L0_cond_setup()
    _L0_cond_in = {k: v for k, v in _L0_cond_all.items() if k in ('W0', 'b0', 'W1', 'b1', 'W2', 'b2', 'weight', 'bias_k')}
    del _L0_cond_all

    def _L0_ffn_setup():
        import jax, jax.numpy as jnp
        import numpy as np
        B, S, D_IN, D_OUT = (2, 256, 512, 512)
        E, K, R = (8, 2, 16)
        SCALING = 32.0 / 16.0
        key = jax.random.key(seed)
        ks = jax.random.split(key, 6)
        x = jax.random.normal(ks[0], (B, S, D_IN), dtype=jnp.float32)
        gate_w = jax.random.normal(ks[1], (E, D_IN), dtype=jnp.float32) * 0.02
        base_w = jax.random.normal(ks[2], (D_OUT, D_IN), dtype=jnp.float32) * 0.02
        base_b = jax.random.normal(ks[3], (D_OUT,), dtype=jnp.float32) * 0.02
        lora_A = jax.random.normal(ks[4], (E, R, D_IN), dtype=jnp.float32) * 0.02
        lora_B = jax.random.normal(ks[5], (E, D_OUT, R), dtype=jnp.float32) * 0.02
        return {'x': x, 'gate_w': gate_w, 'base_w': base_w, 'base_b': base_b, 'lora_A': lora_A, 'lora_B': lora_B}
    _L0_ffn_all = _L0_ffn_setup()
    _L0_ffn_in = {k: v for k, v in _L0_ffn_all.items() if k in ('gate_w', 'base_w', 'base_b', 'lora_A', 'lora_B')}
    del _L0_ffn_all

    def _L1_cond_setup():
        import jax, jax.numpy as jnp
        import numpy as np
        from jax import lax
        N, C_IN, L = (32, 32, 512)
        C_OUT, K, GROUPS = (32, 9, 4)
        C_DIM, PAD, STRIDE = (128, 4, 1)
        key = jax.random.key(seed)
        k1, k2, k3, k4, k5 = jax.random.split(key, 5)
        x = jax.random.normal(k1, (N, C_IN, L), dtype=jnp.float32)
        c = jax.random.normal(k2, (N, C_DIM), dtype=jnp.float32)
        weight = jax.random.normal(k3, (C_OUT, C_IN // GROUPS, K), dtype=jnp.float32)
        c_weight = jax.random.normal(k4, (C_OUT, C_DIM), dtype=jnp.float32)
        bias = jax.random.normal(k5, (C_OUT,), dtype=jnp.float32)
        return {'x': x, 'c': c, 'weight': weight, 'c_weight': c_weight, 'bias': bias}
    _L1_cond_all = _L1_cond_setup()
    _L1_cond_in = {k: v for k, v in _L1_cond_all.items() if k in ('weight', 'c_weight')}
    del _L1_cond_all

    def _L1_ffn_setup():
        import jax, jax.numpy as jnp
        import numpy as np
        LORA_SCALE = 16.0 / jnp.sqrt(16.0)
        TOP_K = 2
        key = jax.random.key(seed)
        k1, k2, k3, k4 = jax.random.split(key, 4)
        B_, S, D, O, E, R = (4, 256, 512, 512, 4, 16)
        x = jax.random.normal(k1, (B_, S, D), dtype=jnp.float32)
        router_w = jax.random.normal(k2, (E, D), dtype=jnp.float32) * 0.02
        A = jax.random.normal(k3, (E, R, D), dtype=jnp.float32) * 0.02
        B = jax.random.normal(k4, (O,), dtype=jnp.float32)
        B = jax.random.normal(k4, (E, O, R), dtype=jnp.float32) * 0.02
        return {'x': x, 'router_w': router_w, 'A': A, 'B': B}
    _L1_ffn_all = _L1_ffn_setup()
    _L1_ffn_in = {k: v for k, v in _L1_ffn_all.items() if k in ('router_w', 'A', 'B')}
    del _L1_ffn_all
    return {'x': x, 'cond_128': cond_128, 'fside_S_0': fside_S_0, 'L0_cond_W0': _L0_cond_in['W0'], 'L0_cond_b0': _L0_cond_in['b0'], 'L0_cond_W1': _L0_cond_in['W1'], 'L0_cond_b1': _L0_cond_in['b1'], 'L0_cond_W2': _L0_cond_in['W2'], 'L0_cond_b2': _L0_cond_in['b2'], 'L0_cond_weight': _L0_cond_in['weight'], 'L0_cond_bias_k': _L0_cond_in['bias_k'], 'L0_ffn_gate_w': _L0_ffn_in['gate_w'], 'L0_ffn_base_w': _L0_ffn_in['base_w'], 'L0_ffn_base_b': _L0_ffn_in['base_b'], 'L0_ffn_lora_A': _L0_ffn_in['lora_A'], 'L0_ffn_lora_B': _L0_ffn_in['lora_B'], 'L1_cond_weight': _L1_cond_in['weight'], 'L1_cond_c_weight': _L1_cond_in['c_weight'], 'L1_ffn_router_w': _L1_ffn_in['router_w'], 'L1_ffn_A': _L1_ffn_in['A'], 'L1_ffn_B': _L1_ffn_in['B']}

def reference(x, cond_128, fside_S_0, L0_cond_W0, L0_cond_b0, L0_cond_W1, L0_cond_b1, L0_cond_W2, L0_cond_b2, L0_cond_weight, L0_cond_bias_k, L0_ffn_gate_w, L0_ffn_base_w, L0_ffn_base_b, L0_ffn_lora_A, L0_ffn_lora_B, L1_cond_weight, L1_cond_c_weight, L1_ffn_router_w, L1_ffn_A, L1_ffn_B):
    import jax
    import jax.numpy as jnp

    def _L0_cond_ref(x, embedding, W0, b0, W1, b1, W2, b2, weight, bias_k):
        import jax, jax.numpy as jnp
        import numpy as np
        K = 8
        T = 1.0
        D_EMBD = 128
        IN_C = 32
        OUT_C = 32
        BS = 32
        H = 512
        HID = 128
        h = jax.nn.gelu(embedding @ W0 + b0, approximate=False)
        h = jax.nn.gelu(h @ W1 + b1, approximate=False)
        att = jax.nn.softmax((h @ W2 + b2) / T, axis=-1)
        agg_w = jnp.einsum('bk,koi->boi', att, weight[..., 0])
        agg_b = att @ bias_k
        out = jnp.einsum('boi,bih->boh', agg_w, x) + agg_b[:, :, None]
        return out

    def _L0_ffn_ref(x, gate_w, base_w, base_b, lora_A, lora_B):
        import jax, jax.numpy as jnp
        import numpy as np
        B, S, D_IN, D_OUT = (2, 256, 512, 512)
        E, K, R = (8, 2, 16)
        SCALING = 32.0 / 16.0
        gate_logits = jnp.einsum('bsd,ed->bse', x, gate_w)
        weights, selected = jax.lax.top_k(gate_logits, K)
        weights = jax.nn.softmax(weights.astype(jnp.float32), axis=2).astype(x.dtype)
        result = jnp.einsum('bsd,od->bso', x, base_w) + base_b
        w_full = jnp.sum(jax.nn.one_hot(selected, E, dtype=x.dtype) * weights[..., None], axis=2)
        low = jnp.einsum('bsd,erd->ebsr', x, lora_A)
        lora_out = jnp.einsum('ebsr,eor,bse->bso', low, lora_B, w_full)
        result = result + SCALING * lora_out
        return result

    def _L1_cond_ref(x, c, weight, c_weight, bias):
        import jax, jax.numpy as jnp
        import numpy as np
        from jax import lax
        N, C_IN, L = (32, 32, 512)
        C_OUT, K, GROUPS = (32, 9, 4)
        C_DIM, PAD, STRIDE = (128, 4, 1)
        out = lax.conv_general_dilated(x, weight, window_strides=(STRIDE,), padding=[(PAD, PAD)], dimension_numbers=('NCH', 'OIH', 'NCH'), feature_group_count=GROUPS)
        ctx = jnp.einsum('nd,od->no', c, c_weight)
        out = out + ctx[:, :, None] + bias[None, :, None]
        return out

    def _L1_ffn_ref(x, router_w, A, B):
        import jax, jax.numpy as jnp
        import numpy as np
        LORA_SCALE = 16.0 / jnp.sqrt(16.0)
        TOP_K = 2
        D = x.shape[-1]
        flat = x.reshape(-1, D)
        logits = flat @ router_w.T
        topk_vals, topk_idx = jax.lax.top_k(logits, TOP_K)
        sparse = jnp.full_like(logits, -jnp.inf)
        rows = jnp.arange(logits.shape[0])[:, None]
        sparse = sparse.at[rows, topk_idx].set(topk_vals)
        gates = jax.nn.softmax(sparse, axis=-1)
        mid = jnp.einsum('tf,erf->ter', flat, A)
        all_deltas = jnp.einsum('ter,eor->teo', mid, B) * LORA_SCALE
        delta = jnp.einsum('te,teo->to', gates, all_deltas)
        return delta.reshape(*x.shape[:-1], -1)
    x = x + _L0_ffn_ref(_L0_cond_ref(x, cond_128, L0_cond_W0, L0_cond_b0, L0_cond_W1, L0_cond_b1, L0_cond_W2, L0_cond_b2, L0_cond_weight, L0_cond_bias_k), L0_ffn_gate_w, L0_ffn_base_w, L0_ffn_base_b, L0_ffn_lora_A, L0_ffn_lora_B)
    x = x + _L1_ffn_ref(_L1_cond_ref(x, cond_128, L1_cond_weight, L1_cond_c_weight, fside_S_0), L1_ffn_router_w, L1_ffn_A, L1_ffn_B)
    return x

_drawn_inputs = setup_inputs


def setup_inputs(seed=0):
    import zlib

    import numpy as np

    out = dict(_drawn_inputs(seed))
    spreads = {'L0_cond_b0': (0.0, 0.8), 'L0_cond_b1': (0.0, 0.491), 'L0_cond_b2': (0.0, 0.515)}
    factors = {'L0_cond_bias_k': 2.88,
     'L0_ffn_gate_w': 3.362,
     'L0_ffn_lora_A': 2.993,
     'L0_ffn_lora_B': 2.933}
    for name, (base, spread) in spreads.items():
        noise = np.random.default_rng([zlib.crc32(name.encode()), seed]).standard_normal(out[name].shape)
        drawn = base * np.exp(spread * noise) if base else spread * noise
        out[name] = jnp.asarray(drawn.astype(out[name].dtype))
    for name, factor in factors.items():
        out[name] = (out[name] * factor).astype(out[name].dtype)
    return out
```

```python
from contextlib import ExitStack

import concourse.bass as bass
from concourse import mybir

F32 = mybir.dt.float32
F32R = mybir.dt.float32r
ALU = mybir.AluOpType
ACT = mybir.ActivationFunctionType
AX_X = mybir.AxisListType.X


def two_layer_mixer(nc: bass.Bass, x, cond, fside, W0, b0, W1, b1, W2, b2, mix_w, mix_b,
                    gate_w, base_w, base_b, lora_A, lora_B, conv_w, ctx_w, router_w, A1, B1, out):
    P = 128
    NB, C, D = x.shape
    TT = NB * C // P
    BT = P // C
    TG = 4
    G = TT // TG
    DC = D // P
    CD = cond.shape[1]
    K0 = W2.shape[1]
    E0, R, _ = lora_A.shape
    ER0 = E0 * R
    LG = ER0 + E0
    E1 = router_w.shape[0]
    ER1 = E1 * R
    PJ = ER1 + E1
    CI, TAPS = conv_w.shape[1:]
    PAD = TAPS // 2
    TA = 5
    TB = TAPS - TA
    SCALE0 = 32.0 / 16.0
    SCALE1 = 16.0 / 16.0 ** 0.5
    assert ER0 == P and 2 * ER1 == P and TA * PJ <= 512 and TG * PJ <= 512 and D == 512

    x_h = x.rearrange("(g t b) c d -> g t (b c) d", g=G, b=BT)
    out_h = out.rearrange("(g t b) c d -> g t (b c) d", g=G, b=BT)

    with ExitStack() as ctx:
        def sb(name, shape, dt=F32):
            return ctx.enter_context(nc.sbuf_tensor(name, shape, dt))

        def sem(name):
            return ctx.enter_context(nc.semaphore(name))

        ident = sb("ident", [P, P])
        ones = sb("ones", [P, P])
        ones_r = sb("ones_r", [P, P], F32R)
        lower = sb("lower", [P, E0, E0])
        same_group = sb("same_group", [P, P // CI])
        x1 = sb("x1", [P, TG, D])
        x1p = sb("x1p", [P, TG, D])
        outb = sb("outb", [P, TG, D])
        cond_s = sb("cond_s", [NB, CD])
        w0_s = sb("w0_s", [P, P])
        w1_s = sb("w1_s", [P, P])
        w2_s = sb("w2_s", [P, K0])
        b0_s = sb("b0_s", [P, 1])
        b1_s = sb("b1_s", [P, 1])
        b2_s = sb("b2_s", [NB, K0])
        mixw_s = x1[0:K0, 0:C * C // D, :].rearrange("k t d -> k (t d)")
        mixb_s = sb("mixb_s", [K0, BT, C])
        base_s = sb("base_s", [P, DC, D])
        baseb_s = sb("baseb_s", [P, D])
        la_s = sb("la_s", [P, D])
        gw_s = sb("gw_s", [E0, D])
        lb_in = x1p[:, 0, :].rearrange("p (e o) -> p e o", e=E0)
        b1e_in = x1p[:, 1, 0:E1 * DC * R].rearrange("p (e o) -> p e o", e=E1)
        lb_s = sb("lb_s", [P, DC, E0, R])
        conv_s = sb("conv_s", [P, CI, TAPS])
        ctxw_s = sb("ctxw_s", [P, CD])
        fside_s = sb("fside_s", [P, 1])
        a1_s = sb("a1_s", [PJ, D + 2 * PAD])
        b1e_s = sb("b1e_s", [P, DC, 2, E1, R])
        condT = sb("condT", [P, NB])
        ctxwT = sb("ctxwT", [P, P])
        h1T = sb("h1T", [P, NB])
        h2T = sb("h2T", [P, NB])
        att_l = sb("att_l", [NB, K0])
        att_m = sb("att_m", [NB, 1])
        att_d = sb("att_d", [NB, K0])
        att_e = sb("att_e", [NB, K0])
        att_s = sb("att_s", [NB, 1])
        att_r = sb("att_r", [NB, 1])
        att = sb("att", [NB, K0])
        attT = sb("attT", [K0, NB])
        mixT = sb("mixT", [P, TT, P])
        mixbias = sb("mixbias", [P, TT])
        ctxbias = sb("ctxbias", [P, TT])
        lgT = sb("lgT", [P, DC, LG])
        lg_sum = sb("lg_sum", [P, LG])
        base_sum = sb("base_sum", [P, D])
        pj_sum = sb("pj_sum", [P, PJ])
        base_h = sb("base_h", [P, DC, D], F32R)
        base_l = sb("base_l", [P, DC, D], F32R)
        lb_h = sb("lb_h", [P, D], F32R)
        lb_l = sb("lb_l", [P, D], F32R)
        pj_h = sb("pj_h", [P, DC, TAPS, PJ], F32R)
        pj_l = sb("pj_l", [P, DC, TAPS, PJ], F32R)
        tapm = outb[:, :, :].rearrange("p t d -> p (t d)")[:, 0:TAPS * P].rearrange("p (k c) -> p k c", c=P)
        tap_h = sb("tap_h", [P, TAPS, P], F32R)
        tap_l = sb("tap_l", [P, TAPS, P], F32R)
        b1e_h = sb("b1e_h", [P, D], F32R)
        b1e_l = sb("b1e_l", [P, D], F32R)
        xr = sb("xr", [P, TG, D])
        xb = sb("xb", [P, TG, D])
        xb_b = sb("xb_b", [P, D])
        c0f = sb("c0f", [P, TG, D])
        c0h = sb("c0h", [P, TG, D], F32R)
        c0l = sb("c0l", [P, TG, D], F32R)
        lgs = sb("lgs", [P, TG, LG])
        lw = sb("lw", [P, TG, ER0])
        lwTh = sb("lwTh", [P, TG * P], F32R)
        lwTl = sb("lwTl", [P, TG * P], F32R)
        x1Th = sb("x1Th", [P, 2, D], F32R)
        x1Tl = sb("x1Tl", [P, 2, D], F32R)
        zh = sb("zh", [P, TG, TAPS, PJ], F32R)
        zl = sb("zl", [P, TG, TAPS, PJ], F32R)
        pj = sb("pj", [P, TG, PJ])
        mw = sb("mw", [P, TG, 2, ER1])
        mwT = sb("mwT", [P, TG * P], F32R)

        def gate_tiles(n, e):
            return dict(top=sb(f"top{n}", [P, TG]), gt=sb(f"gt{n}", [P, TG, e, e]),
                        eq=sb(f"eq{n}", [P, TG, e, e]), rank=sb(f"rank{n}", [P, TG, e]),
                        dif=sb(f"dif{n}", [P, TG, e]), ex=sb(f"ex{n}", [P, TG, e]),
                        kept=sb(f"kept{n}", [P, TG, e]), tot=sb(f"tot{n}", [P, TG]),
                        inv=sb(f"inv{n}", [P, TG]), w=sb(f"w{n}", [P, TG, e]))

        gate0 = gate_tiles(0, E0)
        gate1 = gate_tiles(1, E1)

        ps = ctx.enter_context(nc.psum_tensor("ps", [P, 8, 512], F32))
        TP0, TP1, ZA, ZB, PR, Y = 0, 1, 2, 3, 4, 5
        MISC = 3
        y_bank = [Y, Y + 1, Y + 2, Y]

        consts = sem("consts")
        const_step = sem("const_step")
        in_cond, in_w0, in_w1, in_w2, in_bias, in_mixw, in_mixb = (
            sem(f"in_{n}") for n in ("cond", "w0", "w1", "w2", "bias", "mixw", "mixb"))
        in_lg, in_base, in_baseb, in_lb, in_conv, in_ctx, in_fside, in_a1, in_b1e = (
            sem(f"in_{n}") for n in ("lg", "base", "baseb", "lb", "conv", "ctx", "fside", "a1", "b1e"))
        x_in = [sem(f"x_in{t}") for t in range(TG)]
        out_done = [sem(f"out_done{t}") for t in range(TG)]
        condT_mm, condT_ok, h1_mm, h1_ok, h2_mm, h2_ok, att_mm = (
            sem(n) for n in ("condT_mm", "condT_ok", "h1_mm", "h1_ok", "h2_mm", "h2_ok", "att_mm"))
        att_step, att_dif, att_exp, att_ok, attT_mm, attT_ok = (
            sem(n) for n in ("att_step", "att_dif", "att_exp", "att_ok", "attT_mm", "attT_ok"))
        mixb_mm, mixb_ok, ctx_mm, ctx_ok, mixw_mm, mixw_a, mixw_v = (
            sem(n) for n in ("mixb_mm", "mixb_ok", "ctx_mm", "ctx_ok", "mixw_mm", "mixw_a", "mixw_v"))
        sum_mm, sum_ok, mix_zero, tap_ok, pad_ok = (
            sem(n) for n in ("sum_mm", "sum_ok", "mix_zero", "tap_ok", "pad_ok"))
        inner_ok = sem("inner_ok")
        prep_mm, prep_hi, prep_ok = sem("prep_mm"), sem("prep_hi"), sem("prep_ok")
        c0_mm, c0_full, c0_hi, c0_lo, lg_mm, lg_out = (
            sem(n) for n in ("c0_mm", "c0_full", "c0_hi", "c0_lo", "lg_mm", "lg_out"))
        gate0_step, dif0_ok, ex0_ok, lw_ok, lwT_mm, lwT_hi, lwT_lo = (
            sem(n) for n in ("gate0_step", "dif0_ok", "ex0_ok", "lw_ok", "lwT_mm", "lwT_hi", "lwT_lo"))
        xb_step, xb_ok, y_mm, x1_ok, x1p_ok = (
            sem(n) for n in ("xb_step", "xb_ok", "y_mm", "x1_ok", "x1p_ok"))
        x1T_mm, x1T_hi, x1T_lo, za_mm, za_hi, za_lo, zb_mm, zb_hi, zb_lo = (
            sem(n) for n in ("x1T_mm", "x1T_hi", "x1T_lo", "za_mm", "za_hi", "za_lo",
                             "zb_mm", "zb_hi", "zb_lo"))
        pj_mm, pj_ok, gate1_step, dif1_ok, ex1_ok, mw_ok, mwT_mm, mwT_hi, mwT_lo, d_mm, out_ok = (
            sem(n) for n in ("pj_mm", "pj_ok", "gate1_step", "dif1_ok", "ex1_ok", "mw_ok",
                             "mwT_mm", "mwT_hi", "mwT_lo", "d_mm", "out_ok"))

        def lg_unit(c0):
            moves = []
            for n, c in enumerate((c0, c0 + 1)):
                moves.append((n * LG, la_s[:, c * P:(c + 1) * P]))
                moves.append((n * LG + ER0, gw_s[:, c * P:(c + 1) * P]))
            return dict(need=[(in_lg, 32)], moves=moves, n=2 * LG,
                        full=lgT[:, c0:c0 + 2, :].rearrange("p c e -> p (c e)"))

        def base_unit(c):
            return dict(need=[(in_base, 16)], n=D, hi=base_h[:, c, :], lo=base_l[:, c, :],
                        moves=[(o * P, base_s[:, o, c * P:(c + 1) * P]) for o in range(DC)])

        def ctxw_unit():
            return dict(need=[(in_ctx, 16)], moves=[(0, ctxw_s[:, :])], full=ctxwT[:, :], n=P)

        def lb_unit():
            return dict(need=[(inner_ok, 1)], n=D, hi=lb_h[:, :], lo=lb_l[:, :], spread=DC,
                        moves=[(o * P, lb_s[:, o, :, :].rearrange("p e r -> p (e r)")) for o in range(DC)])

        def pj_unit(c, k0, k1):
            return dict(need=[(in_a1, 32), (pad_ok, 1)], n=(k1 - k0) * PJ,
                        hi=pj_h[:, c, k0:k1, :].rearrange("p k e -> p (k e)"),
                        lo=pj_l[:, c, k0:k1, :].rearrange("p k e -> p (k e)"),
                        moves=[((k - k0) * PJ, a1_s[:, c * P + 2 * PAD - k:c * P + 2 * PAD - k + P])
                               for k in range(k0, k1)])

        def tap_unit(k0, k1):
            return dict(need=[(tap_ok, TAPS)], n=(k1 - k0) * P,
                        hi=tap_h[:, k0:k1, :].rearrange("p k e -> p (k e)"),
                        lo=tap_l[:, k0:k1, :].rearrange("p k e -> p (k e)"),
                        moves=[((k - k0) * P, tapm[:, k, :]) for k in range(k0, k1)])

        def b1e_unit():
            return dict(need=[(inner_ok, 3)], n=D, hi=b1e_h[:, :], lo=b1e_l[:, :], spread=DC,
                        moves=[(o * P, b1e_s[:, o, :, :, :].rearrange("p a e r -> p (a e r)"))
                               for o in range(DC)])

        units = [lg_unit(0), lg_unit(2), ctxw_unit()]
        N0 = len(units)
        units += [base_unit(c) for c in range(DC)] + [lb_unit()]
        units += [pj_unit(c, *k) for c in range(DC) for k in ((0, TA), (TA, TAPS))]
        units += [tap_unit(k, k + 3) for k in range(0, TAPS, 3)] + [b1e_unit()]
        N1 = len(units)
        PREP_BANKS = (TP1, ZA, Y, Y + 1, Y + 2)
        for n, u in enumerate(units):
            u["bank"] = (TP0, TP1, ZA)[n] if n < N0 else PREP_BANKS[(n - N0) % len(PREP_BANKS)]
            before = [m for m in range(n) if units[m]["bank"] == u["bank"]]
            u["after"] = before[-1] + 1 if before else 0
            u["his"] = sum("hi" in v for v in units[:n + 1])
            u["src"] = ps[:, u["bank"], 0:u["n"]]
            if "spread" in u:
                u["src"] = u["src"].rearrange("p (o q) -> p q o", o=u["spread"])
                u["hi"], u["lo"] = (v.rearrange("p (q o) -> p q o", o=u["spread"]) for v in (u["hi"], u["lo"]))
        NB_, NPJ = N0 + DC, N0 + DC + 1 + 2 * DC
        late = list(range(N0, N1))
        late.insert(late.index(NB_) + 2, "base_sum")
        late.insert(late.index(NPJ) + 1, "pj_sum")
        shares = [late[len(late) * t // TG:len(late) * (t + 1) // TG] for t in range(TG)]

        def copy_mix_blocks(copy, quads):
            for q in quads:
                for j in range(BT):
                    src = ps[q * C:(q + 1) * C, PR, :].rearrange("p (m n) -> p m n", n=NB)[:, :, j:NB:BT]
                    last = copy(mixT[j * C:(j + 1) * C, :, j * C + q:(j + 1) * C:BT], src.rearrange("p m n -> p n m"))
            return last

        block = ctx.enter_context(nc.Block())

        @block.sync
        def _(sp):
            def load_x(g, t):
                sp.dma_start(xr[:, t, :], x_h[g, t]).then_inc(x_in[t], 16)

            def refill(g):
                for t in range(TG):
                    sp.wait_ge(c0_mm, TG * (g - 1) + t + 1)
                    sp.wait_ge(xb_ok, TG * (g - 1) + t + 1)
                    load_x(g, t)

            def store(g):
                for t in range(TG):
                    sp.wait_ge(out_ok, TG * (g + 1) + t + 1)
                    sp.dma_start(out_h[g, t], outb[:, t, :]).then_inc(out_done[t], 16)

            sp.dma_start(cond_s[:, :], cond).then_inc(in_cond, 16)
            sp.dma_start(w0_s[:, :], W0).then_inc(in_w0, 16)
            sp.dma_start(w1_s[:, :], W1).then_inc(in_w1, 16)
            sp.dma_start(la_s[:, :], lora_A.rearrange("e r d -> (e r) d")).then_inc(in_lg, 16)
            sp.dma_start(gw_s[:, :], gate_w).then_inc(in_lg, 16)
            sp.dma_start(mixw_s[:, :], mix_w.rearrange("k o i a -> k (o i a)")).then_inc(in_mixw, 16)
            sp.dma_start(mixb_s[:, :, :], mix_b.unsqueeze(1).to_broadcast([K0, BT, C])).then_inc(in_mixb, 16)
            sp.dma_start(ctxw_s[:, :], ctx_w.partition_broadcast(BT)).then_inc(in_ctx, 16)
            load_x(0, 0)
            sp.dma_start(base_s[:, :, :], base_w.rearrange("(o p) d -> p o d", p=P)).then_inc(in_base, 16)
            load_x(0, 1)
            load_x(0, 2)
            sp.dma_start(lb_in, lora_B.rearrange("e (p o) r -> p e (o r)", p=P)).then_inc(in_lb, 16)
            load_x(0, 3)
            sp.dma_start(a1_s[0:ER1, PAD:PAD + D], A1.rearrange("e r d -> (e r) d")).then_inc(in_a1, 16)
            sp.dma_start(a1_s[ER1:PJ, PAD:PAD + D], router_w).then_inc(in_a1, 16)
            sp.dma_start(b1e_in, B1.rearrange("e (p o) r -> p e (o r)", p=P)).then_inc(in_b1e, 16)
            for t in range(TG):
                sp.sem_inc(out_done[t], 16)
            refill(1)
            with nc.sync.Fori(1, G - 1) as i:
                refill(i + 1)
                store(i - 1)
            store(G - 2)
            store(G - 1)
            for t in range(TG):
                sp.wait_ge(out_done[t], 16 * (G + 1))

        @block.gpsimd
        def _(pool):
            nc.gpsimd.memset(ident[:, :], 0.0).then_inc(const_step, 1)
            for j in range(BT):
                pool.dma_start(fside_s[j * C:(j + 1) * C, :], fside.rearrange("(p a) -> p a", a=1)).then_inc(in_fside, 16)
            pool.wait_ge(const_step, 1)
            nc.gpsimd.affine_select(out=ident[:, :], in_=ident[:, :], compare_op=ALU.not_equal, fill=1.0,
                                    base=0, pattern=[[-1, P]], channel_multiplier=1).then_inc(consts, 1)
            nc.gpsimd.memset(mixT[:, :, :], 0.0).then_inc(mix_zero, 1)
            pool.dma_start(baseb_s[:, :], base_b.partition_broadcast(P)).then_inc(in_baseb, 16)
            for j in range(BT):
                pool.dma_start(conv_s[j * C:(j + 1) * C, :, :], conv_w).then_inc(in_conv, 16)
            nc.gpsimd.memset(ones[:, :], 1.0).then_inc(consts, 1)
            nc.gpsimd.memset(ones_r[:, :].bitcast(F32), 1.0).then_inc(consts, 1)
            nc.gpsimd.memset(lower[:, :, :], 1.0).then_inc(const_step, 1)
            pool.wait_ge(const_step, 2)
            nc.gpsimd.affine_select(out=lower[:, :, :], in_=lower[:, :, :], compare_op=ALU.is_gt, fill=0.0,
                                    base=0, pattern=[[1, E0], [-1, E0]], channel_multiplier=0).then_inc(consts, 1)
            nc.gpsimd.memset(a1_s[:, 0:PAD], 0.0)
            nc.gpsimd.memset(a1_s[:, PAD + D:D + 2 * PAD], 0.0).then_inc(pad_ok, 1)
            nc.gpsimd.memset(same_group[:, :], 1.0).then_inc(const_step, 1)
            pool.wait_ge(const_step, 3)
            nc.gpsimd.affine_select(out=same_group[:, :], in_=same_group[:, :], compare_op=ALU.is_ge, fill=0.0,
                                    base=0, pattern=[[-CI, P // CI]], channel_multiplier=1).then_inc(const_step, 1)
            pool.wait_ge(const_step, 4)
            nc.gpsimd.affine_select(out=same_group[:, :], in_=same_group[:, :], compare_op=ALU.is_ge, fill=0.0,
                                    base=CI - 1, pattern=[[CI, P // CI]], channel_multiplier=-1).then_inc(const_step, 1)
            pool.wait_ge(const_step, 5)
            pool.wait_ge(in_conv, 16 * BT)
            for k in range(TAPS):
                nc.gpsimd.tensor_tensor(tapm[:, k, :].rearrange("p (g c) -> p g c", c=CI),
                                        conv_s[:, :, k].unsqueeze(1).to_broadcast([P, P // CI, CI]),
                                        same_group[:, :].unsqueeze(2).to_broadcast([P, P // CI, CI]),
                                        ALU.mult).then_inc(tap_ok, 1)

            def keep_x1(i, t):
                nc.gpsimd.tensor_copy(x1p[:, t, :], x1[:, t, :]).then_inc(x1p_ok, 1)

            def bias_x(i, t, l1):
                pool.wait_ge(x_in[t], 16 * (i + 1))
                if l1:
                    pool.wait_ge(out_ok, TG * (i - 1) + t + 1)
                    pool.wait_ge(x1_ok, TG * (i - 1) + t + 1)
                nc.gpsimd.tensor_tensor(xb[:, t, :], xr[:, t, :], baseb_s[:, :], ALU.add).then_inc(xb_step, 1)
                if l1:
                    keep_x1(i, t)
                nc.gpsimd.tensor_tensor(xb_b[:, :], base_sum[:, :],
                                        mixbias[:, bass.ds(TG * i + t, 1)].to_broadcast([P, D]),
                                        ALU.mult).then_inc(xb_step, 1)
                pool.wait_ge(xb_step, 2 * (TG * i + t) + 2)
                nc.gpsimd.tensor_tensor(xb[:, t, :], xb[:, t, :], xb_b[:, :], ALU.add).then_inc(xb_ok, 1)
                pool.wait_ge(xb_ok, TG * i + t + 1)

            pool.wait_ge(in_baseb, 16)
            pool.wait_ge(sum_ok, 2)
            pool.wait_ge(mixb_ok, 1)
            for t in range(TG):
                bias_x(0, t, False)
            with nc.gpsimd.Fori(1, G) as i:
                for t in range(TG):
                    bias_x(i, t, True)
            for t in range(TG):
                pool.wait_ge(out_ok, TG * (G - 1) + t + 1)
                pool.wait_ge(x1_ok, TG * (G - 1) + t + 1)
                keep_x1(G, t)

        @block.scalar
        def _(act):
            act.dma_start(b0_s[:, :], b0.rearrange("(p a) -> p a", a=1)).then_inc(in_bias, 16)
            act.dma_start(b1_s[:, :], b1.rearrange("(p a) -> p a", a=1)).then_inc(in_bias, 16)
            act.dma_start(w2_s[:, :], W2).then_inc(in_w2, 16)
            act.dma_start(b2_s[:, :], b2.partition_broadcast(NB)).then_inc(in_bias, 16)

            def prep(n):
                u = units[n]
                if "hi" in u:
                    act.wait_ge(prep_mm, n + 1)
                    nc.scalar.activation(u["hi"], u["src"], ACT.Copy).then_inc(prep_hi, 1)

            act.wait_ge(h1_mm, 1)
            act.wait_ge(in_bias, 48)
            nc.scalar.activation(h1T[:, :], ps[:, MISC, 0:NB], ACT.Gelu, bias=b0_s[:, :]).then_inc(h1_ok, 1)
            act.wait_ge(h2_mm, 1)
            nc.scalar.activation(h2T[:, :], ps[:, MISC, 0:NB], ACT.Gelu, bias=b1_s[:, :]).then_inc(h2_ok, 1)
            act.wait_ge(att_dif, 1)
            nc.scalar.activation(att_e[:, :], att_d[:, :], ACT.Exp).then_inc(att_exp, 1)
            act.wait_ge(mixw_mm, 1)
            act.wait_ge(mix_zero, 1)
            copy_mix_blocks(nc.scalar.copy, (0, 1)).then_inc(mixw_a, 1)
            act.wait_ge(sum_mm, 1)
            nc.scalar.activation(lg_sum[:, :], ps[:, MISC, 0:LG], ACT.Copy).then_inc(sum_ok, 1)

            def late_step(n):
                if n == "base_sum":
                    act.wait_ge(sum_mm, 2)
                    nc.scalar.activation(base_sum[:, :], ps[:, MISC, 0:D], ACT.Copy).then_inc(sum_ok, 1)
                elif n == "pj_sum":
                    act.wait_ge(sum_mm, 3)
                    nc.scalar.activation(pj_sum[:, :], ps[:, MISC, 0:PJ], ACT.Copy).then_inc(sum_ok, 1)
                else:
                    prep(n)

            def phase1(i, l0, l1, shares=None):
                p = i - 1
                for t in range(TG):
                    if l0:
                        act.wait_ge(c0_mm, TG * i + t + 1)
                        nc.scalar.activation(c0f[:, t, :], ps[:, TP0, :], ACT.Copy).then_inc(c0_full, 1)
                    for n in (shares[t] if shares else ()):
                        late_step(n)
                    if l1:
                        if t + 1 < TG:
                            act.wait_ge(x1T_mm, TG * p + t + 2)
                            nc.scalar.activation(x1Th[:, (t + 1) % 2, :], ps[:, TP1, :], ACT.Copy).then_inc(x1T_hi, 1)
                        act.wait_ge(za_mm, TG * p + t + 1)
                        nc.scalar.activation(zh[:, t, 0:TA, :].rearrange("p k e -> p (k e)"),
                                             ps[:, ZA, 0:TA * PJ], ACT.Copy).then_inc(za_hi, 1)
                        act.wait_ge(zb_mm, TG * p + t + 1)
                        nc.scalar.activation(zh[:, t, TA:TAPS, :].rearrange("p k e -> p (k e)"),
                                             ps[:, ZB, 0:TB * PJ], ACT.Copy).then_inc(zb_hi, 1)

            def phase2(i, l0, l1):
                if l0:
                    act.wait_ge(dif0_ok, i + 1)
                    nc.scalar.activation(gate0["ex"][:, :, :], gate0["dif"][:, :, :], ACT.Exp).then_inc(ex0_ok, 1)
                if l1:
                    act.wait_ge(dif1_ok, i)
                    nc.scalar.activation(gate1["ex"][:, :, :], gate1["dif"][:, :, :], ACT.Exp).then_inc(ex1_ok, 1)
                if l0:
                    act.wait_ge(lwT_mm, i + 1)
                    nc.scalar.activation(lwTh[:, :], ps[:, TP0, :], ACT.Copy).then_inc(lwT_hi, 1)
                if l1:
                    act.wait_ge(mwT_mm, i)
                    nc.scalar.activation(mwT[:, :], ps[:, TP1, :], ACT.Copy).then_inc(mwT_hi, 1)
                if l0:
                    act.wait_ge(x1T_mm, TG * i + 1)
                    nc.scalar.activation(x1Th[:, 0, :], ps[:, TP1, :], ACT.Copy).then_inc(x1T_hi, 1)

            phase1(0, True, False, shares)
            phase2(0, True, False)
            with nc.scalar.Fori(1, G) as i:
                phase1(i, True, True)
                phase2(i, True, True)
            phase1(G, False, True)
            phase2(G, False, True)

        @block.vector
        def _(dve):
            def prep(n):
                u = units[n]
                if "hi" in u:
                    dve.wait_ge(prep_hi, u["his"])
                    nc.vector.tensor_tensor(u["lo"], u["src"], u["hi"].bitcast(F32), ALU.subtract).then_inc(prep_ok, 1)
                else:
                    dve.wait_ge(prep_mm, n + 1)
                    nc.vector.tensor_copy(u["full"], u["src"]).then_inc(prep_ok, 1)

            steps = [0]

            def att_do(ins):
                steps[0] += 1
                ins.then_inc(att_step, 1)
                dve.wait_ge(att_step, steps[0])

            dve.wait_ge(condT_mm, 1)
            nc.vector.tensor_copy(condT[:, :], ps[:, MISC, 0:NB]).then_inc(condT_ok, 1)
            dve.wait_ge(att_mm, 1)
            dve.wait_ge(in_bias, 48)
            att_do(nc.vector.tensor_tensor(att_l[:, :], ps[0:NB, MISC, 0:K0], b2_s[:, :], ALU.add))
            att_do(nc.vector.reduce_max(att_m[:, :], att_l[:, :], AX_X))
            nc.vector.tensor_scalar(att_d[:, :], att_l[:, :], att_m[:, 0:1], None, ALU.subtract).then_inc(att_dif, 1)
            dve.wait_ge(att_exp, 1)
            att_do(nc.vector.reduce_sum(att_s[:, :], att_e[:, :], AX_X))
            att_do(nc.vector.reciprocal(att_r[:, :], att_s[:, :]))
            nc.vector.tensor_scalar(att[:, :], att_e[:, :], att_r[:, 0:1], None, ALU.mult).then_inc(att_ok, 1)
            prep(0)
            prep(1)
            prep(2)
            dve.wait_ge(attT_mm, 1)
            nc.vector.tensor_copy(attT[:, :], ps[0:K0, MISC, 0:NB]).then_inc(attT_ok, 1)
            dve.wait_ge(mixw_mm, 1)
            dve.wait_ge(mix_zero, 1)
            copy_mix_blocks(nc.vector.tensor_copy, (2, 3)).then_inc(mixw_v, 1)
            dve.wait_ge(mixb_mm, 1)
            for j in range(BT):
                last = nc.vector.tensor_copy(mixbias[j * C:(j + 1) * C, :], ps[j * C:(j + 1) * C, MISC, j:NB:BT])
            last.then_inc(mixb_ok, 1)
            dve.wait_ge(ctx_mm, 1)
            dve.wait_ge(in_fside, 16 * BT)
            for j in range(BT):
                rows = slice(j * C, (j + 1) * C)
                last = nc.vector.tensor_scalar(ctxbias[rows, :], ps[rows, MISC, j:NB:BT], fside_s[rows, 0:1],
                                               None, ALU.add)
            last.then_inc(ctx_ok, 1)
            dve.wait_ge(consts, 4)
            dve.wait_ge(mixb_ok, 1)
            dve.wait_ge(sum_ok, 1)

            def gates(i, g, logits, e, scale, step_sem, dif_ok, ex_ok, n0, out_w):
                count = [0]

                def step(ins):
                    count[0] += 1
                    ins.then_inc(step_sem, 1)
                    dve.wait_ge(step_sem, n0 + count[0])

                per_f = logits.unsqueeze(2).to_broadcast([P, TG, e, e])
                per_e = logits.unsqueeze(3).to_broadcast([P, TG, e, e])
                step(nc.vector.reduce_max(g["top"][:, :], logits, AX_X))
                nc.vector.tensor_tensor(g["dif"][:, :, :], logits,
                                        g["top"][:, :].unsqueeze(2).to_broadcast([P, TG, e]),
                                        ALU.subtract).then_inc(dif_ok, 1)
                nc.vector.tensor_tensor(g["gt"][:, :, :, :], per_f, per_e, ALU.is_gt)
                step(nc.vector.tensor_tensor(g["eq"][:, :, :, :], per_f, per_e, ALU.is_equal))
                low = lower[:, 0:e, 0:e].unsqueeze(1).to_broadcast([P, TG, e, e])
                step(nc.vector.tensor_tensor(g["eq"][:, :, :, :], g["eq"][:, :, :, :], low, ALU.mult))
                step(nc.vector.tensor_tensor(g["gt"][:, :, :, :], g["gt"][:, :, :, :], g["eq"][:, :, :, :], ALU.add))
                step(nc.vector.reduce_sum(g["rank"][:, :, :], g["gt"][:, :, :, :], AX_X))
                dve.wait_ge(ex_ok, i)
                step(nc.vector.scalar_tensor_tensor(out=g["kept"][:, :, :], in0=g["rank"][:, :, :], scalar=2.0,
                                                    in1=g["ex"][:, :, :], op0=ALU.is_lt, op1=ALU.mult))
                step(nc.vector.reduce_sum(g["tot"][:, :], g["kept"][:, :, :], AX_X))
                step(nc.vector.reciprocal(g["inv"][:, :], g["tot"][:, :]))
                step(nc.vector.scalar_tensor_tensor(out=g["w"][:, :, :], in0=g["kept"][:, :, :], scalar=scale,
                                                    in1=g["inv"][:, :].unsqueeze(2).to_broadcast([P, TG, e]),
                                                    op0=ALU.mult, op1=ALU.mult))
                assert count[0] == GATE_STEPS

            GATE_STEPS = 9

            def minus_hi(lo, bank, hi):
                return nc.vector.tensor_tensor(lo, bank, hi.bitcast(F32), ALU.subtract)

            dve.wait_ge(in_lb, 16)
            nc.vector.tensor_copy(lb_s[:, :, :, :], lb_in.rearrange("p e (o r) -> p o e r", r=R)).then_inc(inner_ok, 1)
            dve.wait_ge(in_b1e, 16)
            for n in range(2):
                nc.vector.tensor_copy(b1e_s[:, :, n, :, :],
                                      b1e_in.rearrange("p e (o r) -> p o e r", r=R)).then_inc(inner_ok, 1)

            def phase1(i, l0, l1, shares=None):
                p = i - 1
                for t in range(TG):
                    if l0:
                        dve.wait_ge(c0_full, TG * i + t + 1)
                        nc.vector.tensor_copy(c0h[:, t, :], c0f[:, t, :]).then_inc(c0_hi, 1)
                        dve.wait_ge(c0_hi, TG * i + t + 1)
                        minus_hi(c0l[:, t, :], c0f[:, t, :], c0h[:, t, :]).then_inc(c0_lo, 1)
                    for n in (shares[t] if shares else ()):
                        if n not in ("base_sum", "pj_sum"):
                            prep(n)
                    if l1:
                        if t + 1 < TG:
                            dve.wait_ge(x1T_hi, TG * p + t + 2)
                            minus_hi(x1Tl[:, (t + 1) % 2, :], ps[:, TP1, :], x1Th[:, (t + 1) % 2, :]).then_inc(x1T_lo, 1)
                        dve.wait_ge(za_hi, TG * p + t + 1)
                        minus_hi(zl[:, t, 0:TA, :].rearrange("p k e -> p (k e)"), ps[:, ZA, 0:TA * PJ],
                                 zh[:, t, 0:TA, :].rearrange("p k e -> p (k e)")).then_inc(za_lo, 1)
                        dve.wait_ge(zb_hi, TG * p + t + 1)
                        minus_hi(zl[:, t, TA:TAPS, :].rearrange("p k e -> p (k e)"), ps[:, ZB, 0:TB * PJ],
                                 zh[:, t, TA:TAPS, :].rearrange("p k e -> p (k e)")).then_inc(zb_lo, 1)
                    if l0:
                        dve.wait_ge(lg_mm, TG * i + t + 1)
                        nc.vector.scalar_tensor_tensor(out=lgs[:, t, :], in0=lg_sum[:, :],
                                                       scalar=mixbias[:, bass.ds(TG * i + t, 1)],
                                                       in1=ps[:, PR, 0:LG], op0=ALU.mult, op1=ALU.add).then_inc(lg_out, 1)

            def phase2(i, l0, l1):
                p = i - 1
                if l0:
                    dve.wait_ge(lg_out, TG * (i + 1))
                    gates(i + 1, gate0, lgs[:, :, ER0:LG], E0, SCALE0, gate0_step, dif0_ok, ex0_ok,
                          GATE_STEPS * i, None)
                    nc.vector.tensor_tensor(lw[:, :, :].rearrange("p t (e r) -> p t e r", r=R),
                                            lgs[:, :, 0:ER0].rearrange("p t (e r) -> p t e r", r=R),
                                            gate0["w"][:, :, :].unsqueeze(3).to_broadcast([P, TG, E0, R]),
                                            ALU.mult).then_inc(lw_ok, 1)
                if l1:
                    dve.wait_ge(pj_mm, i)
                    for t in range(TG):
                        nc.vector.scalar_tensor_tensor(out=pj[:, t, :], in0=pj_sum[:, :],
                                                       scalar=ctxbias[:, bass.ds(TG * p + t, 1)],
                                                       in1=ps[:, PR, t * PJ:(t + 1) * PJ],
                                                       op0=ALU.mult, op1=ALU.add).then_inc(pj_ok, 1)
                    dve.wait_ge(pj_ok, TG * i)
                    gates(i, gate1, pj[:, :, ER1:PJ], E1, SCALE1, gate1_step, dif1_ok, ex1_ok,
                          GATE_STEPS * p, None)
                    for n in range(2):
                        last = nc.vector.tensor_tensor(mw[:, :, n, :].rearrange("p t (e r) -> p t e r", r=R),
                                                       pj[:, :, 0:ER1].rearrange("p t (e r) -> p t e r", r=R),
                                                       gate1["w"][:, :, :].unsqueeze(3).to_broadcast([P, TG, E1, R]),
                                                       ALU.mult)
                    last.then_inc(mw_ok, 1)
                if l0:
                    dve.wait_ge(lwT_hi, i + 1)
                    minus_hi(lwTl[:, :], ps[:, TP0, :], lwTh[:, :]).then_inc(lwT_lo, 1)

                def make_x1(t):
                    dve.wait_ge(y_mm, TG * i + t + 1)
                    dve.wait_ge(xb_ok, TG * i + t + 1)
                    if l1:
                        dve.wait_ge(x1p_ok, TG * p + t + 1)
                    nc.vector.tensor_tensor(x1[:, t, :], ps[:, y_bank[t], :], xb[:, t, :], ALU.add).then_inc(x1_ok, 1)

                def make_out(t):
                    dve.wait_ge(d_mm, TG * p + t + 1)
                    dve.wait_ge(x1p_ok, TG * p + t + 1)
                    dve.wait_ge(out_done[t], 16 * i)
                    nc.vector.tensor_tensor(outb[:, t, :], ps[:, ZA + t % 2, :], x1p[:, t, :], ALU.add).then_inc(out_ok, 1)

                if l0:
                    for t in range(TG - 1):
                        make_x1(t)
                if l1:
                    dve.wait_ge(mwT_hi, i)
                    minus_hi(mwT[ER1:P, :], ps[ER1:P, TP1, :], mwT[ER1:P, :]).then_inc(mwT_lo, 1)
                    make_out(0)
                if l0:
                    dve.wait_ge(x1T_hi, TG * i + 1)
                    minus_hi(x1Tl[:, 0, :], ps[:, TP1, :], x1Th[:, 0, :]).then_inc(x1T_lo, 1)
                if l1:
                    make_out(1)
                if l0:
                    make_x1(TG - 1)
                if l1:
                    make_out(2)
                    make_out(3)

            dve.sem_inc(out_ok, TG)
            phase1(0, True, False, shares)
            dve.wait_ge(sum_ok, 3)
            phase2(0, True, False)
            with nc.vector.Fori(1, G) as i:
                phase1(i, True, True)
                phase2(i, True, True)
            phase1(G, False, True)
            phase2(G, False, True)

        @block.tensor
        def _(pe):
            def prep(n):
                u = units[n]
                for s, v in u["need"]:
                    pe.wait_ge(s, v)
                if u["after"]:
                    pe.wait_ge(prep_ok, u["after"])
                for col, src in u["moves"]:
                    rows, cols = src.shape
                    last = nc.tensor.transpose(ps[0:cols, u["bank"], col:col + rows], src, ident[0:rows, 0:rows])
                last.then_inc(prep_mm, 1)

            pe.wait_ge(consts, 1)
            pe.wait_ge(in_cond, 16)
            nc.tensor.transpose(ps[:, MISC, 0:NB], cond_s[:, :], ident[0:NB, 0:NB]).then_inc(condT_mm, 1)
            pe.wait_ge(in_w0, 16)
            pe.wait_ge(condT_ok, 1)
            nc.tensor.matmul(ps[:, MISC, 0:NB], w0_s[:, :], condT[:, :], start=True, stop=True).then_inc(h1_mm, 1)
            pe.wait_ge(in_w1, 16)
            pe.wait_ge(h1_ok, 1)
            nc.tensor.matmul(ps[:, MISC, 0:NB], w1_s[:, :], h1T[:, :], start=True, stop=True).then_inc(h2_mm, 1)
            pe.wait_ge(in_w2, 16)
            pe.wait_ge(h2_ok, 1)
            nc.tensor.matmul(ps[0:NB, MISC, 0:K0], h2T[:, :], w2_s[:, :], start=True, stop=True).then_inc(att_mm, 1)
            for n in range(N0):
                prep(n)
            pe.wait_ge(att_ok, 1)
            nc.tensor.transpose(ps[0:K0, MISC, 0:NB], att[:, :], ident[0:NB, 0:NB]).then_inc(attT_mm, 1)
            pe.wait_ge(attT_ok, 1)
            pe.wait_ge(in_mixw, 16)
            by_rest = mixw_s[:, :].rearrange("k (m q) -> k m q", q=P)
            for m in range(C * C // P):
                last = nc.tensor.matmul(ps[:, PR, m * NB:(m + 1) * NB], by_rest[:, m, :], attT[:, :],
                                        start=True, stop=True)
            last.then_inc(mixw_mm, 1)
            pe.wait_ge(in_mixb, 16)
            nc.tensor.matmul(ps[:, MISC, 0:NB], mixb_s[:, :, :].rearrange("k j o -> k (j o)"), attT[:, :],
                             start=True, stop=True).then_inc(mixb_mm, 1)
            pe.wait_ge(prep_ok, N0)
            pe.wait_ge(mixb_ok, 1)
            nc.tensor.matmul(ps[:, MISC, 0:NB], ctxwT[:, :], condT[:, :], start=True, stop=True).then_inc(ctx_mm, 1)
            pe.wait_ge(consts, 2)
            pe.wait_ge(ctx_ok, 1)
            for c in range(DC):
                last = nc.tensor.matmul(ps[:, MISC, 0:LG], ones[:, :], lgT[:, c, :], start=c == 0, stop=c == DC - 1)
            last.then_inc(sum_mm, 1)
            pe.wait_ge(mixw_a, 1)
            pe.wait_ge(mixw_v, 1)

            def hi_lo(dst, stationary, moving, start=True, stop=True):
                n = len(stationary)
                for c in range(n):
                    (sh, sl), (mh, ml) = stationary[c], moving[c]
                    nc.tensor.matmul(dst, sh, mh, start=start and c == 0, stop=False)
                    end = stop and c == n - 1
                    last = nc.tensor.matmul(dst, sh, ml, start=False, stop=end and sl is None)
                    if sl is not None:
                        last = nc.tensor.matmul(dst, sl, mh, start=False, stop=end)
                return last

            def transpose_x1(t):
                for c in range(DC):
                    last = nc.tensor.transpose(ps[:, TP1, c * P:(c + 1) * P], x1[:, t, c * P:(c + 1) * P], ident[:, :])
                last.then_inc(x1T_mm, 1)

            def project_x1(t, bank, k0, k1):
                s = t % 2
                cols = [slice(c * P, (c + 1) * P) for c in range(DC)]
                return hi_lo(ps[:, bank, 0:(k1 - k0) * PJ],
                             [(x1Th[:, s, c], x1Tl[:, s, c]) for c in cols],
                             [(pj_h[:, c, k0:k1, :].rearrange("p k e -> p (k e)"),
                               pj_l[:, c, k0:k1, :].rearrange("p k e -> p (k e)")) for c in range(DC)])

            def base(t):
                cols = [slice(c * P, (c + 1) * P) for c in range(DC)]
                hi_lo(ps[:, y_bank[t], :], [(c0h[:, t, c], c0l[:, t, c]) for c in cols],
                      [(base_h[:, c, :], base_l[:, c, :]) for c in range(DC)], stop=False)

            def experts0(t):
                cols = slice(t * P, (t + 1) * P)
                hi_lo(ps[:, y_bank[t], :], [(lwTh[:, cols], lwTl[:, cols])], [(lb_h[:, :], lb_l[:, :])],
                      start=False).then_inc(y_mm, 1)

            def experts1(t):
                cols = slice(t * P, (t + 1) * P)
                nc.tensor.matmul(ps[:, ZA + t % 2, :], mwT[:, cols], b1e_h[:, :], start=True, stop=False)
                nc.tensor.matmul(ps[:, ZA + t % 2, :], mwT[:, cols], b1e_l[:, :], start=False,
                                 stop=True).then_inc(d_mm, 1)

            def late_step(n):
                if n == "base_sum":
                    pe.wait_ge(consts, 3)
                    pe.wait_ge(prep_ok, NB_)
                    pe.wait_ge(sum_ok, 1)
                    hi_lo(ps[:, MISC, 0:D], [(ones_r[:, :], None)] * DC,
                          [(base_h[:, c, :], base_l[:, c, :]) for c in range(DC)]).then_inc(sum_mm, 1)
                elif n == "pj_sum":
                    pe.wait_ge(prep_ok, NPJ)
                    pe.wait_ge(sum_ok, 2)
                    hi_lo(ps[:, MISC, 0:PJ], [(ones_r[:, :], None)] * DC,
                          [(pj_h[:, c, PAD, :], pj_l[:, c, PAD, :]) for c in range(DC)]).then_inc(sum_mm, 1)
                else:
                    prep(n)

            def phase1(i, l0, l1, shares=None):
                p = i - 1
                for t in range(TG):
                    if l0:
                        pe.wait_ge(x_in[t], 16 * (i + 1))
                        if t:
                            pe.wait_ge(c0_full, TG * i + t)
                        for c in range(DC):
                            last = nc.tensor.matmul(ps[:, TP0, c * P:(c + 1) * P], xr[:, t, c * P:(c + 1) * P],
                                                    mixT[:, bass.ds(TG * i + t, 1), :].rearrange("p a o -> p (a o)"),
                                                    start=True, stop=True)
                        last.then_inc(c0_mm, 1)
                    for n in (shares[t] if shares else ()):
                        late_step(n)
                    if l1:
                        pe.wait_ge(x1T_lo, TG * p + t + 1)
                        if t + 1 < TG:
                            transpose_x1(t + 1)
                        if t:
                            pe.wait_ge(za_lo, TG * p + t)
                        else:
                            pe.wait_ge(out_ok, TG * p + 3)
                        project_x1(t, ZA, 0, TA).then_inc(za_mm, 1)
                        if t:
                            pe.wait_ge(zb_lo, TG * p + t)
                        else:
                            pe.wait_ge(out_ok, TG * p + 4)
                        project_x1(t, ZB, TA, TAPS).then_inc(zb_mm, 1)
                    if l0:
                        pe.wait_ge(c0_full, TG * i + t + 1)
                        if t:
                            pe.wait_ge(lg_out, TG * i + t)
                        for c in range(DC):
                            last = nc.tensor.matmul(ps[:, PR, 0:LG], c0f[:, t, c * P:(c + 1) * P], lgT[:, c, :],
                                                    start=c == 0, stop=c == DC - 1)
                        last.then_inc(lg_mm, 1)
                if shares:
                    pe.wait_ge(prep_ok, N1)

            def phase2(i, l0, l1):
                p = i - 1
                if l0:
                    pe.wait_ge(c0_lo, TG * i + 1)
                    base(0)
                if l1:
                    pe.wait_ge(zb_lo, TG * i)
                    if l0:
                        pe.wait_ge(lg_out, TG * (i + 1))
                    hi_lo(ps[:, PR, 0:TG * PJ], [(tap_h[:, k, :], tap_l[:, k, :]) for k in range(TAPS)],
                          [(zh[:, :, k, :], zl[:, :, k, :]) for k in range(TAPS)]).then_inc(pj_mm, 1)
                if l0:
                    pe.wait_ge(c0_lo, TG * i + 2)
                    base(1)
                    pe.wait_ge(lw_ok, i + 1)
                    for t in range(TG):
                        last = nc.tensor.transpose(ps[:, TP0, t * P:(t + 1) * P], lw[:, t, :], ident[:, :])
                    last.then_inc(lwT_mm, 1)
                    pe.wait_ge(c0_lo, TG * i + 3)
                    base(2)
                    pe.wait_ge(lwT_lo, i + 1)
                    for t in range(TG - 1):
                        experts0(t)
                if l1:
                    pe.wait_ge(mw_ok, i)
                    for t in range(TG):
                        last = nc.tensor.transpose(ps[:, TP1, t * P:(t + 1) * P],
                                                   mw[:, t, :, :].rearrange("p a e -> p (a e)"), ident[:, :])
                    last.then_inc(mwT_mm, 1)
                if l0:
                    pe.wait_ge(c0_lo, TG * i + 4)
                    pe.wait_ge(x1_ok, TG * i + 1)
                    base(3)
                if l1:
                    pe.wait_ge(mwT_lo, i)
                    experts1(0)
                if l0:
                    transpose_x1(0)
                if l1:
                    experts1(1)
                if l0:
                    experts0(3)
                if l1:
                    for t in (2, 3):
                        pe.wait_ge(out_ok, TG * i + t - 1)
                        experts1(t)

            phase1(0, True, False, shares)
            phase2(0, True, False)
            with nc.tensor.Fori(1, G) as i:
                phase1(i, True, True)
                phase2(i, True, True)
            phase1(G, False, True)
            phase2(G, False, True)


_INS = ["x", "cond_128", "fside_S_0", "L0_cond_W0", "L0_cond_b0", "L0_cond_W1", "L0_cond_b1", "L0_cond_W2",
        "L0_cond_b2", "L0_cond_weight", "L0_cond_bias_k", "L0_ffn_gate_w", "L0_ffn_base_w", "L0_ffn_base_b",
        "L0_ffn_lora_A", "L0_ffn_lora_B", "L1_cond_weight", "L1_cond_c_weight", "L1_ffn_router_w",
        "L1_ffn_A", "L1_ffn_B"]
_OUTS = [((64, 32, 512), "float32")]


def kernel(**inputs):
    import numpy as _np
    import concourse.bacc as _bacc
    from concourse import mybir as _mybir
    from concourse.bass_utils import run_bass_kernel_spmd as _run

    nc = _bacc.Bacc("TRN2", target_bir_lowering=False, num_devices=1)
    arrays, args = {}, []
    for name in _INS:
        a = _np.ascontiguousarray(inputs[name])
        arrays[f"in_{name}_dram"] = a
        args.append(nc.dram_tensor(f"in_{name}_dram", a.shape, _mybir.dt.from_np(a.dtype), kind="ExternalInput").ap())
    for i, (shape, dtype) in enumerate(_OUTS):
        dt = _mybir.dt.from_np(_np.dtype(dtype))
        args.append(nc.dram_tensor(f"out_{i}_dram", shape, dt, kind="ExternalOutput").ap())
    two_layer_mixer(nc, *args)
    r = _run(nc, [arrays], core_ids=[0])
    return r.results[0]["out_0_dram"]
```

```python
from contextlib import ExitStack

import concourse.bass as bass
from concourse import mybir

F32 = mybir.dt.float32
F32R = mybir.dt.float32r
ALU = mybir.AluOpType
ACT = mybir.ActivationFunctionType
AX_X = mybir.AxisListType.X


def two_layer_mixer(nc: bass.Bass, x, cond, fside, W0, b0, W1, b1, W2, b2, mix_w, mix_b,
                    gate_w, base_w, base_b, lora_A, lora_B, conv_w, ctx_w, router_w, A1, B1, out):
    P = 128
    NB, C, D = x.shape
    TT = NB * C // P
    BT = P // C
    TG = 4
    G = TT // TG
    DC = D // P
    CD = cond.shape[1]
    K0 = W2.shape[1]
    E0, R, _ = lora_A.shape
    ER0 = E0 * R
    LG = ER0 + E0
    E1 = router_w.shape[0]
    ER1 = E1 * R
    PJ = ER1 + E1
    CI, TAPS = conv_w.shape[1:]
    PAD = TAPS // 2
    TA = 5
    TB = TAPS - TA
    SCALE0 = 32.0 / 16.0
    SCALE1 = 16.0 / 16.0 ** 0.5
    assert ER0 == P and 2 * ER1 == P and TA * PJ <= 512 and TG * PJ <= 512 and D == 512

    x_h = x.rearrange("(g t b) c d -> g t (b c) d", g=G, b=BT)
    out_h = out.rearrange("(g t b) c d -> g t (b c) d", g=G, b=BT)

    with ExitStack() as ctx:
        def sb(name, shape, dt=F32):
            return ctx.enter_context(nc.sbuf_tensor(name, shape, dt))

        def sem(name):
            return ctx.enter_context(nc.semaphore(name))

        ident = sb("ident", [P, P])
        ones = sb("ones", [P, P])
        ones_r = sb("ones_r", [P, P], F32R)
        lower = sb("lower", [P, E0, E0])
        same_group = sb("same_group", [P, P // CI])
        x1 = sb("x1", [P, TG, D])
        x1p = sb("x1p", [P, TG, D])
        outb = sb("outb", [P, TG, D])
        cond_s = sb("cond_s", [NB, CD])
        w0_s = sb("w0_s", [P, P])
        w1_s = sb("w1_s", [P, P])
        w2_s = sb("w2_s", [P, K0])
        b0_s = sb("b0_s", [P, 1])
        b1_s = sb("b1_s", [P, 1])
        b2_s = sb("b2_s", [1, K0])
        mixw_s = x1[0:K0, 0:C * C // D, :].rearrange("k t d -> k (t d)")
        mixb_s = sb("mixb_s", [K0, BT, C])
        base_s = sb("base_s", [P, DC, D])
        baseb_s = sb("baseb_s", [P, D])
        la_s = sb("la_s", [P, D])
        gw_s = sb("gw_s", [E0, D])
        lb_in = x1p[:, 0, :].rearrange("p (e o) -> p e o", e=E0)
        b1e_in = x1p[:, 1, 0:E1 * DC * R].rearrange("p (e o) -> p e o", e=E1)
        lb_s = sb("lb_s", [P, DC, E0, R])
        conv_s = sb("conv_s", [P, CI, TAPS])
        ctxw_s = sb("ctxw_s", [P, CD])
        fside_s = sb("fside_s", [P, 1])
        a1_s = sb("a1_s", [PJ, D + 2 * PAD])
        b1e_s = sb("b1e_s", [P, DC, 2, E1, R])
        warm = sb("warm", [P, 1])
        condT = sb("condT", [P, NB])
        ctxwT = sb("ctxwT", [P, P])
        h1T = sb("h1T", [P, NB])
        h2T = sb("h2T", [P, NB])
        att_m = sb("att_m", [NB, 1])
        att_e = sb("att_e", [NB, K0])
        att_s = sb("att_s", [NB, 1])
        att_r = sb("att_r", [NB, 1])
        att3 = sb("att3", [NB, 3, 32])
        att3T = sb("att3T", [P, NB], F32R)
        attT = sb("attT", [K0, NB])
        mixT = sb("mixT", [P, TT, P])
        mixbias = sb("mixbias", [P, TT])
        ctxbias = sb("ctxbias", [P, TT])
        lgT = sb("lgT", [P, DC, LG])
        lg_sum = sb("lg_sum", [P, LG])
        base_sum = sb("base_sum", [P, D])
        pj_sum = sb("pj_sum", [P, PJ])
        base_h = sb("base_h", [P, DC, D], F32R)
        base_l = sb("base_l", [P, DC, D], F32R)
        lb_h = sb("lb_h", [P, D], F32R)
        lb_l = sb("lb_l", [P, D], F32R)
        pj_h = sb("pj_h", [P, DC, TAPS, PJ], F32R)
        pj_l = sb("pj_l", [P, DC, TAPS, PJ], F32R)
        tapm = outb[:, :, :].rearrange("p t d -> p (t d)")[:, 0:TAPS * P].rearrange("p (k c) -> p k c", c=P)
        tap_h = sb("tap_h", [P, TAPS, P], F32R)
        tap_l = sb("tap_l", [P, TAPS, P], F32R)
        b1e_h = sb("b1e_h", [P, D], F32R)
        b1e_l = sb("b1e_l", [P, D], F32R)
        xr = sb("xr", [P, TG, D])
        xb = sb("xb", [P, TG, D])
        c0f = sb("c0f", [P, TG, D])
        c0h = sb("c0h", [P, TG, D], F32R)
        c0l = sb("c0l", [P, TG, D], F32R)
        lgs = sb("lgs", [P, TG, LG])
        lw = sb("lw", [P, TG, ER0])
        lwTh = sb("lwTh", [P, TG * P], F32R)
        lwTl = sb("lwTl", [P, TG * P], F32R)
        x1Th = sb("x1Th", [P, 2, D], F32R)
        x1Tl = sb("x1Tl", [P, 2, D], F32R)
        zh = sb("zh", [P, TG, TAPS, PJ], F32R)
        zl = sb("zl", [P, TG, TAPS, PJ], F32R)
        mixw3 = zh[:, :, :, :].rearrange("p t k e -> p (t k e)")[:, 0:C * C]
        pj_ctx = sb("pj_ctx", [P, TG, PJ])
        pj = sb("pj", [P, TG, PJ])
        mw = sb("mw", [P, TG, ER1])
        mwT = sb("mwT", [P, TG * P], F32R)

        def gate_tiles(n, e):
            return dict(top=sb(f"top{n}", [P, TG]), above=sb(f"above{n}", [P, TG, e, 2, e]),
                        eq=sb(f"eq{n}", [P, TG, e, e]), rank=sb(f"rank{n}", [P, TG, e]),
                        dif=sb(f"dif{n}", [P, TG, e]), ex=sb(f"ex{n}", [P, TG, e]),
                        kept=sb(f"kept{n}", [P, TG, e]), tot=sb(f"tot{n}", [P, TG]),
                        inv=sb(f"inv{n}", [P, TG]), w=sb(f"w{n}", [P, TG, e]))

        gate0 = gate_tiles(0, E0)
        gate1 = gate_tiles(1, E1)

        ps = ctx.enter_context(nc.psum_tensor("ps", [P, 8, 512], F32))
        TP0, TP1, ZA, ZB, PR, Y = 0, 1, 2, 3, 4, 5
        MISC = 3
        y_bank = [Y, Y + 1, Y + 2, Y]

        def z_banks(t, l0):
            return (ZA, ZB) if l0 or t % 2 else (Y, Y + 1)

        def d_bank(t, l0):
            return ZA + t % 2 if l0 else ZA + t if t < 2 else Y + t - 2

        consts = sem("consts")
        const_step = sem("const_step")
        in_cond, in_w0, in_b0, in_w1, in_b1, in_w2, in_b2, in_mixw, in_mixb = (
            sem(f"in_{n}") for n in ("cond", "w0", "b0", "w1", "b1", "w2", "b2", "mixw", "mixb"))
        in_lg, in_base, in_baseb, in_lb, in_conv, in_ctx, in_fside, in_a1, in_b1e = (
            sem(f"in_{n}") for n in ("lg", "base", "baseb", "lb", "conv", "ctx", "fside", "a1", "b1e"))
        x_in = [sem(f"x_in{t}") for t in range(TG)]
        out_done = [sem(f"out_done{t}") for t in range(TG)]
        condT_mm, condT_ok, h1_mm, h1_ok, h2_mm, h2_ok, att_mm = (
            sem(n) for n in ("condT_mm", "condT_ok", "h1_mm", "h1_ok", "h2_mm", "h2_ok", "att_mm"))
        att_max, att_exp, att_inv, att_ok, att3_zero, attT_mm, att3_hi, att3_ok, attT_ok = (
            sem(n) for n in ("att_max", "att_exp", "att_inv", "att_ok", "att3_zero", "attT_mm",
                             "att3_hi", "att3_ok", "attT_ok"))
        mixw3_zero, mixw3_hi, mixw3_ok, warm_ok, lgT_mm, lg_ok = (
            sem(n) for n in ("mixw3_zero", "mixw3_hi", "mixw3_ok", "warm_ok", "lgT_mm", "lg_ok"))
        mixb_mm, mixb_ok, ctx_mm, ctx_ok, mixw_mm, mixw_a, mixw_v = (
            sem(n) for n in ("mixb_mm", "mixb_ok", "ctx_mm", "ctx_ok", "mixw_mm", "mixw_a", "mixw_v"))
        sum_mm, sum_ok, mix_zero, tap_ok, pad_ok = (
            sem(n) for n in ("sum_mm", "sum_ok", "mix_zero", "tap_ok", "pad_ok"))
        inner_ok = sem("inner_ok")
        prep_mm, prep_hi, prep_ok = sem("prep_mm"), sem("prep_hi"), sem("prep_ok")
        c0_mm, c0_full, c0_hi, c0_lo, lg_mm, lg_out = (
            sem(n) for n in ("c0_mm", "c0_full", "c0_hi", "c0_lo", "lg_mm", "lg_out"))
        gate0_step, dif0_ok, ex0_ok, lw_ok, lwT_mm, lwT_hi, lwT_lo = (
            sem(n) for n in ("gate0_step", "dif0_ok", "ex0_ok", "lw_ok", "lwT_mm", "lwT_hi", "lwT_lo"))
        bias_ok, xb_step, xb_ok, y_mm, x1_ok, x1p_ok, pj_ctx_ok = (
            sem(n) for n in ("bias_ok", "xb_step", "xb_ok", "y_mm", "x1_ok", "x1p_ok", "pj_ctx_ok"))
        x1T_mm, x1T_hi, x1T_lo, za_mm, za_hi, za_lo, zb_mm, zb_hi, zb_lo = (
            sem(n) for n in ("x1T_mm", "x1T_hi", "x1T_lo", "za_mm", "za_hi", "za_lo",
                             "zb_mm", "zb_hi", "zb_lo"))
        pj_mm, pj_ok, gate1_step, dif1_ok, ex1_ok, mw_ok, mwT_mm, mwT_hi, mwT_lo, d_mm, out_ok = (
            sem(n) for n in ("pj_mm", "pj_ok", "gate1_step", "dif1_ok", "ex1_ok", "mw_ok",
                             "mwT_mm", "mwT_hi", "mwT_lo", "d_mm", "out_ok"))

        def lg_unit(c0):
            moves = []
            for n, c in enumerate((c0, c0 + 1)):
                moves.append((n * LG, la_s[:, c * P:(c + 1) * P]))
                moves.append((n * LG + ER0, gw_s[:, c * P:(c + 1) * P]))
            return dict(need=[(in_lg, 32)], moves=moves, n=2 * LG,
                        full=lgT[:, c0:c0 + 2, :].rearrange("p c e -> p (c e)"))

        def base_unit(c):
            return dict(need=[(in_base, 16)], n=D, hi=base_h[:, c, :], lo=base_l[:, c, :],
                        moves=[(o * P, base_s[:, o, c * P:(c + 1) * P]) for o in range(DC)])

        def ctxw_unit():
            return dict(need=[(in_ctx, 16)], moves=[(0, ctxw_s[:, :])], full=ctxwT[:, :], n=P)

        def lb_unit():
            return dict(need=[(inner_ok, 1)], n=D, hi=lb_h[:, :], lo=lb_l[:, :], spread=DC,
                        moves=[(o * P, lb_s[:, o, :, :].rearrange("p e r -> p (e r)")) for o in range(DC)])

        def pj_unit(c, k0, k1):
            return dict(need=[(in_a1, 32), (pad_ok, 1)], n=(k1 - k0) * PJ,
                        hi=pj_h[:, c, k0:k1, :].rearrange("p k e -> p (k e)"),
                        lo=pj_l[:, c, k0:k1, :].rearrange("p k e -> p (k e)"),
                        moves=[((k - k0) * PJ, a1_s[:, c * P + 2 * PAD - k:c * P + 2 * PAD - k + P])
                               for k in range(k0, k1)])

        def tap_unit(k0, k1):
            return dict(need=[(tap_ok, TAPS)], n=(k1 - k0) * P,
                        hi=tap_h[:, k0:k1, :].rearrange("p k e -> p (k e)"),
                        lo=tap_l[:, k0:k1, :].rearrange("p k e -> p (k e)"),
                        moves=[((k - k0) * P, tapm[:, k, :]) for k in range(k0, k1)])

        def b1e_unit():
            return dict(need=[(inner_ok, 3)], n=D, hi=b1e_h[:, :], lo=b1e_l[:, :], spread=DC,
                        moves=[(o * P, b1e_s[:, o, :, :, :].rearrange("p a e r -> p (a e r)"))
                               for o in range(DC)])

        lg_units = [lg_unit(0), lg_unit(2)]
        for u, bank in zip(lg_units, (TP0, ZA)):
            u["bank"], u["src"] = bank, ps[:, bank, 0:u["n"]]
        units = [base_unit(c) for c in range(DC)] + [ctxw_unit(), lb_unit()]
        units += [pj_unit(c, *k) for c in range(DC) for k in ((0, TA), (TA, TAPS))]
        N2 = len(units)
        units += [tap_unit(k, k + 3) for k in range(0, TAPS, 3)] + [b1e_unit()]
        N1 = len(units)
        PREP_BANKS = (TP1, ZA, Y, Y + 2, Y + 1)
        for n, u in enumerate(units):
            if n < N2:
                u["bank"] = PREP_BANKS[(n - N2 + 2) % len(PREP_BANKS)]
            else:
                u["bank"] = PREP_BANKS[(n - N2) % 2]
            before = [m for m in range(n) if units[m]["bank"] == u["bank"]]
            u["after"] = before[-1] + 1 if before else 0
            u["his"] = sum("hi" in v for v in units[:n + 1])
            u["src"] = ps[:, u["bank"], 0:u["n"]]
            if "spread" in u:
                u["src"] = u["src"].rearrange("p (o q) -> p q o", o=u["spread"])
                u["hi"], u["lo"] = (v.rearrange("p (q o) -> p q o", o=u["spread"]) for v in (u["hi"], u["lo"]))
        NBASE, NCTX, NPJ = DC, DC + 1, DC + 2 + 2 * DC
        late = list(range(N2))
        late.insert(late.index(NCTX) + 5, "ctx")
        late.insert(late.index(NBASE) + 3, "base_sum")
        shares = [late[len(late) * t // TG:len(late) * (t + 1) // TG] for t in range(TG)]
        assert N1 == N2 + 4 and "base_sum" in shares[1]

        def copy_mix_blocks(copy, quads, tiles):
            for q in quads:
                for j in range(BT):
                    src = ps[q * C:(q + 1) * C, PR, :].rearrange("p (m n) -> p m n", n=NB)[:, :, j:NB:BT][:, :, tiles]
                    last = copy(mixT[j * C:(j + 1) * C, tiles, j * C + q:(j + 1) * C:BT], src.rearrange("p m n -> p n m"))
            return last

        def mw_half(where, half, a):
            rows = slice(half * ER1, (half + 1) * ER1)
            if where is ps:
                return ps[rows, TP1, 0:TG // 2 * P].rearrange("p (q n) -> p q n", n=P)
            return mwT[rows, :].rearrange("p (q a n) -> p q a n", a=2, n=P)[:, :, a, :]

        block = ctx.enter_context(nc.Block())

        @block.sync
        def _(sp):
            def load_x(g, t):
                sp.dma_start(xr[:, t, :], x_h[g, t]).then_inc(x_in[t], 16)

            def refill(g):
                for t in range(TG):
                    sp.wait_ge(c0_mm, TG * (g - 1) + t + 1)
                    sp.wait_ge(xb_ok, TG * (g - 1) + t + 1)
                    load_x(g, t)

            def store(g):
                for t in range(TG):
                    sp.wait_ge(out_ok, TG * (g + 1) + t + 1)
                    sp.dma_start(out_h[g, t], outb[:, t, :]).then_inc(out_done[t], 16)

            sp.dma_start(cond_s[:, :], cond).then_inc(in_cond, 16)
            sp.dma_start(w0_s[:, :], W0).then_inc(in_w0, 16)
            sp.dma_start(b0_s[:, :], b0.rearrange("(p a) -> p a", a=1)).then_inc(in_b0, 16)
            sp.dma_start(mixw_s[:, :], mix_w.rearrange("k o i a -> k (o i a)")).then_inc(in_mixw, 16)
            sp.dma_start(w1_s[:, :], W1).then_inc(in_w1, 16)
            sp.dma_start(b1_s[:, :], b1.rearrange("(p a) -> p a", a=1)).then_inc(in_b1, 16)
            sp.dma_start(w2_s[:, :], W2).then_inc(in_w2, 16)
            sp.dma_start(b2_s[:, :], b2.rearrange("(a k) -> a k", a=1)).then_inc(in_b2, 16)
            sp.dma_start(la_s[:, :], lora_A.rearrange("e r d -> (e r) d")).then_inc(in_lg, 16)
            sp.dma_start(gw_s[:, :], gate_w).then_inc(in_lg, 16)
            load_x(0, 0)
            sp.dma_start(mixb_s[:, :, :], mix_b.unsqueeze(1).to_broadcast([K0, BT, C])).then_inc(in_mixb, 16)
            sp.dma_start(base_s[:, :, :], base_w.rearrange("(o p) d -> p o d", p=P)).then_inc(in_base, 16)
            load_x(0, 1)
            sp.dma_start(ctxw_s[:, :], ctx_w.partition_broadcast(BT)).then_inc(in_ctx, 16)
            load_x(0, 2)
            sp.dma_start(lb_in, lora_B.rearrange("e (p o) r -> p e (o r)", p=P)).then_inc(in_lb, 16)
            load_x(0, 3)
            sp.dma_start(a1_s[0:ER1, PAD:PAD + D], A1.rearrange("e r d -> (e r) d")).then_inc(in_a1, 16)
            sp.dma_start(a1_s[ER1:PJ, PAD:PAD + D], router_w).then_inc(in_a1, 16)
            sp.dma_start(conv_s[:, :, :], conv_w.partition_broadcast(BT)).then_inc(in_conv, 16)
            sp.dma_start(fside_s[:, :], fside.rearrange("(p a) -> p a", a=1).partition_broadcast(BT)).then_inc(in_fside, 16)
            sp.dma_start(b1e_in, B1.rearrange("e (p o) r -> p e (o r)", p=P)).then_inc(in_b1e, 16)
            for t in range(TG):
                sp.sem_inc(out_done[t], 16)
            refill(1)
            with nc.sync.Fori(1, G - 1) as i:
                refill(i + 1)
                store(i - 1)
            store(G - 2)
            store(G - 1)
            for t in range(TG):
                sp.wait_ge(out_done[t], 16 * (G + 1))

        @block.gpsimd
        def _(pool):
            nc.gpsimd.memset(warm[:, :], 0.0).then_inc(warm_ok, 1)
            nc.gpsimd.memset(ident[:, :], 0.0).then_inc(const_step, 1)
            pool.wait_ge(const_step, 1)
            nc.gpsimd.affine_select(out=ident[:, :], in_=ident[:, :], compare_op=ALU.not_equal, fill=1.0,
                                    base=0, pattern=[[-1, P]], channel_multiplier=1).then_inc(consts, 1)
            nc.gpsimd.memset(ones[:, :], 1.0).then_inc(consts, 1)
            nc.gpsimd.memset(ones_r[:, :].bitcast(F32), 1.0).then_inc(consts, 1)
            nc.gpsimd.memset(mixw3.bitcast(F32), 0.0).then_inc(mixw3_zero, 1)
            nc.gpsimd.memset(att3[:, :, :], 0.0).then_inc(att3_zero, 1)
            nc.gpsimd.memset(mixT[:, :, :], 0.0).then_inc(mix_zero, 1)
            nc.gpsimd.memset(lower[:, :, :], 1.0).then_inc(const_step, 1)
            pool.wait_ge(const_step, 2)
            nc.gpsimd.affine_select(out=lower[:, :, :], in_=lower[:, :, :], compare_op=ALU.is_gt, fill=0.0,
                                    base=0, pattern=[[1, E0], [-1, E0]], channel_multiplier=0).then_inc(consts, 1)
            nc.gpsimd.memset(a1_s[:, 0:PAD], 0.0)
            nc.gpsimd.memset(a1_s[:, PAD + D:D + 2 * PAD], 0.0).then_inc(pad_ok, 1)
            nc.gpsimd.memset(same_group[:, :], 1.0).then_inc(const_step, 1)
            pool.wait_ge(const_step, 3)
            nc.gpsimd.affine_select(out=same_group[:, :], in_=same_group[:, :], compare_op=ALU.is_ge, fill=0.0,
                                    base=0, pattern=[[-CI, P // CI]], channel_multiplier=1).then_inc(const_step, 1)
            pool.wait_ge(const_step, 4)
            nc.gpsimd.affine_select(out=same_group[:, :], in_=same_group[:, :], compare_op=ALU.is_ge, fill=0.0,
                                    base=CI - 1, pattern=[[CI, P // CI]], channel_multiplier=-1).then_inc(const_step, 1)
            pool.dma_start(baseb_s[:, :], base_b.partition_broadcast(P)).then_inc(in_baseb, 16)
            pool.wait_ge(in_lb, 16)
            nc.gpsimd.tensor_copy(lb_s[:, :, :, :], lb_in.rearrange("p e (o r) -> p o e r", r=R)).then_inc(inner_ok, 1)
            pool.wait_ge(const_step, 5)
            pool.wait_ge(in_conv, 16)
            for k in range(TAPS):
                nc.gpsimd.tensor_tensor(tapm[:, k, :].rearrange("p (g c) -> p g c", c=CI),
                                        conv_s[:, :, k].unsqueeze(1).to_broadcast([P, P // CI, CI]),
                                        same_group[:, :].unsqueeze(2).to_broadcast([P, P // CI, CI]),
                                        ALU.mult).then_inc(tap_ok, 1)

            pool.wait_ge(in_b1e, 16)
            for n in range(2):
                nc.gpsimd.tensor_copy(b1e_s[:, :, n, :, :],
                                      b1e_in.rearrange("p e (o r) -> p o e r", r=R)).then_inc(inner_ok, 1)

            def bias_x(i, t):
                pool.wait_ge(x_in[t], 16 * (i + 1))
                pool.wait_ge(bias_ok, TG * i + t + 1)
                nc.gpsimd.tensor_tensor(xb[:, t, :], xb[:, t, :], xr[:, t, :], ALU.add).then_inc(xb_step, 1)
                pool.wait_ge(xb_step, TG * i + t + 1)
                nc.gpsimd.tensor_tensor(xb[:, t, :], xb[:, t, :], baseb_s[:, :], ALU.add).then_inc(xb_ok, 1)

            def context(p, after):
                if after:
                    pool.wait_ge(pj_ok, p)
                nc.gpsimd.tensor_tensor(pj_ctx[:, :, :], pj_sum[:, :].unsqueeze(1).to_broadcast([P, TG, PJ]),
                                        ctxbias[:, bass.ds(TG * p, TG)].unsqueeze(2).to_broadcast([P, TG, PJ]),
                                        ALU.mult).then_inc(pj_ctx_ok, 1)

            pool.wait_ge(in_baseb, 16)
            for t in range(TG):
                bias_x(0, t)
            pool.wait_ge(sum_ok, 3)
            pool.wait_ge(ctx_ok, 1)
            context(0, False)
            with nc.gpsimd.Fori(1, G) as i:
                for t in range(TG):
                    bias_x(i, t)
                context(i, True)

        @block.scalar
        def _(act):
            def prep(n):
                u = units[n]
                if "hi" in u:
                    act.wait_ge(prep_mm, n + 1)
                    nc.scalar.activation(u["hi"], u["src"], ACT.Copy).then_inc(prep_hi, 1)

            act.wait_ge(warm_ok, 1)
            nc.scalar.activation(warm[:, :], warm[:, :], ACT.Gelu)
            act.wait_ge(in_b0, 16)
            act.wait_ge(h1_mm, 1)
            nc.scalar.activation(h1T[:, :], ps[:, MISC, 0:NB], ACT.Gelu, bias=b0_s[:, :]).then_inc(h1_ok, 1)
            act.wait_ge(in_b1, 16)
            act.wait_ge(h2_mm, 1)
            nc.scalar.activation(h2T[:, :], ps[:, MISC, 0:NB], ACT.Gelu, bias=b1_s[:, :]).then_inc(h2_ok, 1)
            act.wait_ge(att_max, 1)
            nc.scalar.activation(att_e[:, :], ps[0:NB, Y, 0:K0], ACT.Exp, bias=att_m[:, :],
                                 accum_out=att_s[:, :]).then_inc(att_exp, 1)
            for n, u in enumerate(lg_units):
                act.wait_ge(lgT_mm, n + 1)
                nc.scalar.activation(u["full"], u["src"], ACT.Copy).then_inc(lg_ok, 1)
            act.wait_ge(mixw_mm, 1)
            act.wait_ge(mix_zero, 1)
            for tiles in (slice(0, TG), slice(TG, TT)):
                copy_mix_blocks(nc.scalar.copy, (0, 1), tiles).then_inc(mixw_a, 1)
            act.wait_ge(sum_mm, 1)
            nc.scalar.activation(lg_sum[:, :], ps[:, MISC, 0:LG], ACT.Copy).then_inc(sum_ok, 1)

            def late_step(n):
                if n == "base_sum":
                    act.wait_ge(sum_mm, 2)
                    nc.scalar.activation(base_sum[:, :], ps[:, MISC, 0:D], ACT.Copy).then_inc(sum_ok, 1)
                elif n == "pj_sum":
                    act.wait_ge(sum_mm, 3)
                    nc.scalar.activation(pj_sum[:, :], ps[:, MISC, 0:PJ], ACT.Copy).then_inc(sum_ok, 1)
                elif n != "ctx":
                    prep(n)

            def bias_term(i, t):
                nc.scalar.activation(xb[:, t, :], base_sum[:, :], ACT.Copy,
                                     scale=mixbias[:, bass.ds(TG * i + t, 1)]).then_inc(bias_ok, 1)

            def keep_x1(i, t):
                act.wait_ge(out_ok, TG * (i - 1) + t + 1)
                act.wait_ge(x1_ok, TG * (i - 1) + t + 1)
                nc.scalar.activation(x1p[:, t, :], x1[:, t, :], ACT.Copy).then_inc(x1p_ok, 1)

            def phase1(i, l0, l1, shares=None):
                p = i - 1
                for t in range(TG):
                    if l0:
                        act.wait_ge(c0_mm, TG * i + t + 1)
                        nc.scalar.activation(c0f[:, t, :], ps[:, TP0, :], ACT.Copy).then_inc(c0_full, 1)
                        nc.scalar.activation(c0h[:, t, :], ps[:, TP0, :], ACT.Copy).then_inc(c0_hi, 1)
                    for n in (shares[t] if shares else ()):
                        late_step(n)
                    if l1:
                        if t + 1 < TG:
                            act.wait_ge(x1T_mm, TG * p + t + 2)
                            nc.scalar.activation(x1Th[:, (t + 1) % 2, :], ps[:, TP1, :], ACT.Copy).then_inc(x1T_hi, 1)
                        za, zb = z_banks(t, l0)
                        act.wait_ge(za_mm, TG * p + t + 1)
                        nc.scalar.activation(zh[:, t, 0:TA, :].rearrange("p k e -> p (k e)"),
                                             ps[:, za, 0:TA * PJ], ACT.Copy).then_inc(za_hi, 1)
                        act.wait_ge(zb_mm, TG * p + t + 1)
                        nc.scalar.activation(zh[:, t, TA:TAPS, :].rearrange("p k e -> p (k e)"),
                                             ps[:, zb, 0:TB * PJ], ACT.Copy).then_inc(zb_hi, 1)
                        keep_x1(i, t)
                        if l0:
                            bias_term(i, t)

            def phase2(i, l0, l1):
                if l0:
                    act.wait_ge(dif0_ok, i + 1)
                    nc.scalar.activation(gate0["ex"][:, :, :], gate0["dif"][:, :, :], ACT.Exp).then_inc(ex0_ok, 1)
                if not l1:
                    act.wait_ge(mixb_ok, 1)
                    act.wait_ge(sum_ok, 2)
                    for t in range(TG):
                        bias_term(0, t)
                    late_step("pj_sum")
                if l1:
                    act.wait_ge(dif1_ok, i)
                    nc.scalar.activation(gate1["ex"][:, :, :], gate1["dif"][:, :, :], ACT.Exp).then_inc(ex1_ok, 1)
                if l0:
                    act.wait_ge(lwT_mm, i + 1)
                    nc.scalar.activation(lwTh[:, :], ps[:, TP0, :], ACT.Copy).then_inc(lwT_hi, 1)
                if not l1:
                    for n in range(N2, N1):
                        prep(n)
                if l1:
                    act.wait_ge(mwT_mm, i)
                    for a in range(2):
                        nc.scalar.activation(mw_half(mwT, 0, a), mw_half(ps, a, a), ACT.Copy).then_inc(mwT_hi, 1)
                if l0:
                    act.wait_ge(x1T_mm, TG * i + 1)
                    nc.scalar.activation(x1Th[:, 0, :], ps[:, TP1, :], ACT.Copy).then_inc(x1T_hi, 1)

            phase1(0, True, False, shares)
            phase2(0, True, False)
            with nc.scalar.Fori(1, G) as i:
                phase1(i, True, True)
                phase2(i, True, True)
            phase1(G, False, True)
            phase2(G, False, True)

        @block.vector
        def _(dve):
            def prep(n):
                u = units[n]
                if "hi" in u:
                    dve.wait_ge(prep_hi, u["his"])
                    nc.vector.tensor_tensor(u["lo"], u["src"], u["hi"].bitcast(F32), ALU.subtract).then_inc(prep_ok, 1)
                else:
                    dve.wait_ge(prep_mm, n + 1)
                    nc.vector.tensor_copy(u["full"], u["src"]).then_inc(prep_ok, 1)

            dve.wait_ge(condT_mm, 1)
            nc.vector.tensor_copy(condT[:, :], ps[:, MISC, 0:NB]).then_inc(condT_ok, 1)
            dve.wait_ge(in_mixw, 16)
            dve.wait_ge(mixw3_zero, 1)
            for n in range(2):
                nc.vector.tensor_copy(mixw3[32 * n:32 * n + K0, :], mixw_s).then_inc(mixw3_hi, 1)
            dve.wait_ge(mixw3_hi, 1)
            nc.vector.tensor_tensor(mixw3[64:64 + K0, :], mixw_s, mixw3[0:K0, :].bitcast(F32),
                                    ALU.subtract).then_inc(mixw3_ok, 1)
            dve.wait_ge(att_mm, 1)
            nc.vector.reduce_max(att_m[:, :], ps[0:NB, Y, 0:K0], AX_X, negate=True).then_inc(att_max, 1)
            dve.wait_ge(att_exp, 1)
            nc.vector.reciprocal(att_r[:, :], att_s[:, :]).then_inc(att_inv, 1)
            dve.wait_ge(att_inv, 1)
            dve.wait_ge(att3_zero, 1)
            nc.vector.tensor_scalar(att3[:, :, 0:K0], att_e[:, :].unsqueeze(1).to_broadcast([NB, 3, K0]),
                                    att_r[:, 0:1], None, ALU.mult).then_inc(att_ok, 1)
            dve.wait_ge(attT_mm, 1)
            nc.vector.tensor_copy(att3T[0:64 + K0, :], ps[0:64 + K0, MISC, 0:NB]).then_inc(att3_hi, 1)
            dve.wait_ge(att3_hi, 1)
            nc.vector.tensor_tensor(att3T[32:32 + K0, :], ps[32:32 + K0, MISC, 0:NB],
                                    att3T[32:32 + K0, :].bitcast(F32), ALU.subtract).then_inc(att3_ok, 1)
            nc.vector.tensor_copy(attT[:, :], ps[0:K0, MISC, 0:NB]).then_inc(attT_ok, 1)
            dve.wait_ge(mixw_mm, 1)
            dve.wait_ge(mix_zero, 1)
            for tiles in (slice(0, TG), slice(TG, TT)):
                copy_mix_blocks(nc.vector.tensor_copy, (2, 3), tiles).then_inc(mixw_v, 1)
            dve.wait_ge(mixb_mm, 1)
            for j in range(BT):
                last = nc.vector.tensor_copy(mixbias[j * C:(j + 1) * C, :], ps[j * C:(j + 1) * C, Y + 1, j:NB:BT])
            last.then_inc(mixb_ok, 1)
            dve.wait_ge(consts, 4)
            dve.wait_ge(mixb_ok, 1)
            dve.wait_ge(sum_ok, 1)

            def gates(i, g, logits, e, scale, step_sem, dif_ok, ex_ok, n0, out_w):
                count = [0]

                def step(ins):
                    count[0] += 1
                    ins.then_inc(step_sem, 1)
                    dve.wait_ge(step_sem, n0 + count[0])

                per_f = logits.unsqueeze(2).to_broadcast([P, TG, e, e])
                per_e = logits.unsqueeze(3).to_broadcast([P, TG, e, e])
                above = g["above"]
                nc.vector.reduce_max(g["top"][:, :], logits, AX_X)
                nc.vector.tensor_tensor(g["eq"][:, :, :, :], per_f, per_e, ALU.is_equal)
                step(nc.vector.tensor_tensor(above[:, :, :, 0, :], per_f, per_e, ALU.is_gt))
                nc.vector.tensor_tensor(g["dif"][:, :, :], logits,
                                        g["top"][:, :].unsqueeze(2).to_broadcast([P, TG, e]),
                                        ALU.subtract).then_inc(dif_ok, 1)
                low = lower[:, 0:e, 0:e].unsqueeze(1).to_broadcast([P, TG, e, e])
                step(nc.vector.tensor_tensor(above[:, :, :, 1, :], g["eq"][:, :, :, :], low, ALU.mult))
                step(nc.vector.reduce_sum(g["rank"][:, :, :], above[:, :, :, :, :].rearrange("p t e a f -> p t e (a f)"), AX_X))
                dve.wait_ge(ex_ok, i)
                step(nc.vector.scalar_tensor_tensor(out=g["kept"][:, :, :], in0=g["rank"][:, :, :], scalar=2.0,
                                                    in1=g["ex"][:, :, :], op0=ALU.is_lt, op1=ALU.mult))
                step(nc.vector.reduce_sum(g["tot"][:, :], g["kept"][:, :, :], AX_X))
                step(nc.vector.reciprocal(g["inv"][:, :], g["tot"][:, :]))
                step(nc.vector.scalar_tensor_tensor(out=g["w"][:, :, :], in0=g["kept"][:, :, :], scalar=scale,
                                                    in1=g["inv"][:, :].unsqueeze(2).to_broadcast([P, TG, e]),
                                                    op0=ALU.mult, op1=ALU.mult))
                assert count[0] == GATE_STEPS

            GATE_STEPS = 7

            def minus_hi(lo, bank, hi):
                return nc.vector.tensor_tensor(lo, bank, hi.bitcast(F32), ALU.subtract)

            def late_step(n):
                if n == "ctx":
                    dve.wait_ge(ctx_mm, 1)
                    dve.wait_ge(in_fside, 16)
                    for j in range(BT):
                        rows = slice(j * C, (j + 1) * C)
                        last = nc.vector.tensor_scalar(ctxbias[rows, :], ps[rows, MISC, j:NB:BT],
                                                       fside_s[rows, 0:1], None, ALU.add)
                    last.then_inc(ctx_ok, 1)
                elif n not in ("base_sum", "pj_sum"):
                    prep(n)

            def phase1(i, l0, l1, shares=None):
                p = i - 1
                for t in range(TG):
                    if l0:
                        dve.wait_ge(c0_hi, TG * i + t + 1)
                        minus_hi(c0l[:, t, :], c0f[:, t, :], c0h[:, t, :]).then_inc(c0_lo, 1)
                    for n in (shares[t] if shares else ()):
                        late_step(n)
                    if l1:
                        if t + 1 < TG:
                            dve.wait_ge(x1T_hi, TG * p + t + 2)
                            minus_hi(x1Tl[:, (t + 1) % 2, :], ps[:, TP1, :], x1Th[:, (t + 1) % 2, :]).then_inc(x1T_lo, 1)
                        za, zb = z_banks(t, l0)
                        dve.wait_ge(za_hi, TG * p + t + 1)
                        minus_hi(zl[:, t, 0:TA, :].rearrange("p k e -> p (k e)"), ps[:, za, 0:TA * PJ],
                                 zh[:, t, 0:TA, :].rearrange("p k e -> p (k e)")).then_inc(za_lo, 1)
                        dve.wait_ge(zb_hi, TG * p + t + 1)
                        minus_hi(zl[:, t, TA:TAPS, :].rearrange("p k e -> p (k e)"), ps[:, zb, 0:TB * PJ],
                                 zh[:, t, TA:TAPS, :].rearrange("p k e -> p (k e)")).then_inc(zb_lo, 1)
                    if l0:
                        dve.wait_ge(lg_mm, TG * i + t + 1)
                        nc.vector.scalar_tensor_tensor(out=lgs[:, t, :], in0=lg_sum[:, :],
                                                       scalar=mixbias[:, bass.ds(TG * i + t, 1)],
                                                       in1=ps[:, PR, 0:LG], op0=ALU.mult, op1=ALU.add).then_inc(lg_out, 1)

            def phase2(i, l0, l1):
                p = i - 1
                if l0:
                    dve.wait_ge(lg_out, TG * (i + 1))
                    gates(i + 1, gate0, lgs[:, :, ER0:LG], E0, SCALE0, gate0_step, dif0_ok, ex0_ok,
                          GATE_STEPS * i, None)
                    nc.vector.tensor_tensor(lw[:, :, :].rearrange("p t (e r) -> p t e r", r=R),
                                            lgs[:, :, 0:ER0].rearrange("p t (e r) -> p t e r", r=R),
                                            gate0["w"][:, :, :].unsqueeze(3).to_broadcast([P, TG, E0, R]),
                                            ALU.mult).then_inc(lw_ok, 1)
                if l1:
                    dve.wait_ge(pj_mm, i)
                    dve.wait_ge(pj_ctx_ok, i)
                    nc.vector.tensor_tensor(pj[:, :, :], ps[:, PR, 0:TG * PJ].rearrange("p (t e) -> p t e", e=PJ),
                                            pj_ctx[:, :, :], ALU.add).then_inc(pj_ok, 1)
                    dve.wait_ge(pj_ok, i)
                    gates(i, gate1, pj[:, :, ER1:PJ], E1, SCALE1, gate1_step, dif1_ok, ex1_ok,
                          GATE_STEPS * p, None)
                    nc.vector.tensor_tensor(mw[:, :, :].rearrange("p t (e r) -> p t e r", r=R),
                                            pj[:, :, 0:ER1].rearrange("p t (e r) -> p t e r", r=R),
                                            gate1["w"][:, :, :].unsqueeze(3).to_broadcast([P, TG, E1, R]),
                                            ALU.mult).then_inc(mw_ok, 1)
                if l0:
                    dve.wait_ge(lwT_hi, i + 1)
                    minus_hi(lwTl[:, :], ps[:, TP0, :], lwTh[:, :]).then_inc(lwT_lo, 1)
                    if not l1:
                        for n in range(N2, N1):
                            prep(n)

                def make_x1(t):
                    dve.wait_ge(y_mm, TG * i + t + 1)
                    dve.wait_ge(xb_ok, TG * i + t + 1)
                    if l1:
                        dve.wait_ge(x1p_ok, TG * p + t + 1)
                    nc.vector.tensor_tensor(x1[:, t, :], ps[:, y_bank[t], :], xb[:, t, :], ALU.add).then_inc(x1_ok, 1)

                def make_out(t):
                    bank = d_bank(t, l0)
                    dve.wait_ge(d_mm, TG * p + t + 1)
                    dve.wait_ge(x1p_ok, TG * p + t + 1)
                    dve.wait_ge(out_done[t], 16 * i)
                    nc.vector.tensor_tensor(outb[:, t, :], ps[:, bank, :], x1p[:, t, :], ALU.add).then_inc(out_ok, 1)

                if l0:
                    for t in range(TG - 1):
                        make_x1(t)
                if l1:
                    for a in range(2):
                        dve.wait_ge(mwT_hi, 2 * p + a + 1)
                        minus_hi(mw_half(mwT, 1, a), mw_half(ps, a, a), mw_half(mwT, 0, a)).then_inc(mwT_lo, 1)
                    make_out(0)
                    make_out(1)
                if l0:
                    dve.wait_ge(x1T_hi, TG * i + 1)
                    minus_hi(x1Tl[:, 0, :], ps[:, TP1, :], x1Th[:, 0, :]).then_inc(x1T_lo, 1)
                if l0:
                    make_x1(TG - 1)
                if l1:
                    make_out(2)
                    make_out(3)

            dve.sem_inc(out_ok, TG)
            phase1(0, True, False, shares)
            phase2(0, True, False)
            with nc.vector.Fori(1, G) as i:
                phase1(i, True, True)
                phase2(i, True, True)
            phase1(G, False, True)
            phase2(G, False, True)

        @block.tensor
        def _(pe):
            def prep(n):
                u = units[n]
                for s, v in u["need"]:
                    pe.wait_ge(s, v)
                if u["after"]:
                    pe.wait_ge(prep_ok, u["after"])
                elif u["bank"] == Y + 1:
                    pe.wait_ge(mixb_ok, 1)
                transposes(u).then_inc(prep_mm, 1)

            def transposes(u):
                for col, src in u["moves"]:
                    rows, cols = src.shape
                    last = nc.tensor.transpose(ps[0:cols, u["bank"], col:col + rows], src, ident[0:rows, 0:rows])
                return last

            def keep_busy(bank, n):
                for _ in range(n):
                    nc.tensor.matmul(ps[:, bank, 0:2 * P], ones_r[:, :], ones_r[:, :].unsqueeze(1).to_broadcast([P, 2, P]), start=True, stop=True)

            pe.wait_ge(consts, 3)
            keep_busy(Y + 2, 7)
            pe.wait_ge(in_cond, 16)
            nc.tensor.transpose(ps[:, MISC, 0:NB], cond_s[:, :], ident[0:NB, 0:NB]).then_inc(condT_mm, 1)
            keep_busy(Y + 2, 2)
            pe.wait_ge(in_w0, 16)
            pe.wait_ge(condT_ok, 1)
            nc.tensor.matmul(ps[:, MISC, 0:NB], w0_s[:, :], condT[:, :], start=True, stop=True).then_inc(h1_mm, 1)
            keep_busy(Y + 2, 4)
            pe.wait_ge(in_w1, 16)
            pe.wait_ge(h1_ok, 1)
            nc.tensor.matmul(ps[:, MISC, 0:NB], w1_s[:, :], h1T[:, :], start=True, stop=True).then_inc(h2_mm, 1)
            keep_busy(Y + 2, 4)
            pe.wait_ge(consts, 2)
            pe.wait_ge(in_b2, 16)
            nc.tensor.matmul(ps[0:NB, Y, 0:K0], ones[0:1, 0:NB], b2_s[:, :], start=True, stop=False)
            pe.wait_ge(in_w2, 16)
            pe.wait_ge(h2_ok, 1)
            nc.tensor.matmul(ps[0:NB, Y, 0:K0], h2T[:, :], w2_s[:, :], start=False, stop=True).then_inc(att_mm, 1)
            keep_busy(Y + 2, 8)
            pe.wait_ge(att_ok, 1)
            nc.tensor.transpose(ps[0:96, MISC, 0:NB], att3[:, :, :].rearrange("b n k -> b (n k)"),
                                ident[0:NB, 0:NB]).then_inc(attT_mm, 1)
            pe.wait_ge(in_lg, 32)
            for u in lg_units:
                transposes(u).then_inc(lgT_mm, 1)
            keep_busy(Y + 2, 3)
            pe.wait_ge(mixw3_ok, 1)
            pe.wait_ge(mixw3_hi, 2)
            pe.wait_ge(att3_ok, 1)
            for m in range(C * C // P):
                last = nc.tensor.matmul(ps[:, PR, m * NB:(m + 1) * NB], mixw3[0:64 + K0, m * P:(m + 1) * P],
                                        att3T[0:64 + K0, :], start=True, stop=True)
            last.then_inc(mixw_mm, 1)
            keep_busy(Y + 2, 2)
            pe.wait_ge(in_mixb, 16)
            pe.wait_ge(attT_ok, 1)
            nc.tensor.matmul(ps[:, Y + 1, 0:NB], mixb_s[:, :, :].rearrange("k j o -> k (j o)"), attT[:, :],
                             start=True, stop=True).then_inc(mixb_mm, 1)
            pe.wait_ge(lg_ok, 2)
            for c in range(DC):
                last = nc.tensor.matmul(ps[:, MISC, 0:LG], ones[:, :], lgT[:, c, :], start=c == 0, stop=c == DC - 1)
            last.then_inc(sum_mm, 1)
            pe.wait_ge(mixw_a, 1)
            pe.wait_ge(mixw_v, 1)

            def hi_lo(dst, stationary, moving, start=True, stop=True):
                n = len(stationary)
                for c in range(n):
                    (sh, sl), (mh, ml) = stationary[c], moving[c]
                    nc.tensor.matmul(dst, sh, mh, start=start and c == 0, stop=False)
                    end = stop and c == n - 1
                    last = nc.tensor.matmul(dst, sh, ml, start=False, stop=end and sl is None)
                    if sl is not None:
                        last = nc.tensor.matmul(dst, sl, mh, start=False, stop=end)
                return last

            def transpose_x1(t):
                for c in range(DC):
                    last = nc.tensor.transpose(ps[:, TP1, c * P:(c + 1) * P], x1[:, t, c * P:(c + 1) * P], ident[:, :])
                last.then_inc(x1T_mm, 1)

            def project_x1(t, bank, k0, k1):
                s = t % 2
                cols = [slice(c * P, (c + 1) * P) for c in range(DC)]
                return hi_lo(ps[:, bank, 0:(k1 - k0) * PJ],
                             [(x1Th[:, s, c], x1Tl[:, s, c]) for c in cols],
                             [(pj_h[:, c, k0:k1, :].rearrange("p k e -> p (k e)"),
                               pj_l[:, c, k0:k1, :].rearrange("p k e -> p (k e)")) for c in range(DC)])

            def base(t):
                cols = [slice(c * P, (c + 1) * P) for c in range(DC)]
                hi_lo(ps[:, y_bank[t], :], [(c0h[:, t, c], c0l[:, t, c]) for c in cols],
                      [(base_h[:, c, :], base_l[:, c, :]) for c in range(DC)], stop=False)

            def experts0(t):
                cols = slice(t * P, (t + 1) * P)
                hi_lo(ps[:, y_bank[t], :], [(lwTh[:, cols], lwTl[:, cols])], [(lb_h[:, :], lb_l[:, :])],
                      start=False).then_inc(y_mm, 1)

            def experts1(t, bank):
                cols = slice(t * P, (t + 1) * P)
                nc.tensor.matmul(ps[:, bank, :], mwT[:, cols], b1e_h[:, :], start=True, stop=False)
                nc.tensor.matmul(ps[:, bank, :], mwT[:, cols], b1e_l[:, :], start=False,
                                 stop=True).then_inc(d_mm, 1)

            def late_step(n):
                if n == "base_sum":
                    pe.wait_ge(consts, 3)
                    pe.wait_ge(prep_ok, NBASE)
                    pe.wait_ge(sum_ok, 1)
                    hi_lo(ps[:, MISC, 0:D], [(ones_r[:, :], None)] * DC,
                          [(base_h[:, c, :], base_l[:, c, :]) for c in range(DC)]).then_inc(sum_mm, 1)
                elif n == "ctx":
                    pe.wait_ge(prep_ok, NCTX)
                    pe.wait_ge(sum_ok, 2)
                    nc.tensor.matmul(ps[:, MISC, 0:NB], ctxwT[:, :], condT[:, :], start=True, stop=True).then_inc(ctx_mm, 1)
                elif n == "pj_sum":
                    pe.wait_ge(prep_ok, NPJ)
                    pe.wait_ge(ctx_ok, 1)
                    hi_lo(ps[:, MISC, 0:PJ], [(ones_r[:, :], None)] * DC,
                          [(pj_h[:, c, PAD, :], pj_l[:, c, PAD, :]) for c in range(DC)]).then_inc(sum_mm, 1)
                else:
                    prep(n)

            def phase1(i, l0, l1, shares=None):
                p = i - 1
                for t in range(TG):
                    if l0:
                        pe.wait_ge(x_in[t], 16 * (i + 1))
                        if t:
                            pe.wait_ge(c0_hi, TG * i + t)
                        for c in range(DC):
                            last = nc.tensor.matmul(ps[:, TP0, c * P:(c + 1) * P], xr[:, t, c * P:(c + 1) * P],
                                                    mixT[:, bass.ds(TG * i + t, 1), :].rearrange("p a o -> p (a o)"),
                                                    start=True, stop=True)
                        last.then_inc(c0_mm, 1)
                    for n in (shares[t] if shares else ()):
                        late_step(n)
                    if l1:
                        pe.wait_ge(x1T_lo, TG * p + t + 1)
                        if t + 1 < TG:
                            transpose_x1(t + 1)
                        za, zb = z_banks(t, l0)
                        if not l0 and t == 0:
                            pe.wait_ge(x1_ok, TG * i)
                        elif t <= (0 if l0 else 1):
                            pe.wait_ge(out_ok, TG * p + 3)
                        elif l0:
                            pe.wait_ge(za_lo, TG * p + t)
                        else:
                            pe.wait_ge(za_lo, TG * p + t - 1)
                        project_x1(t, za, 0, TA).then_inc(za_mm, 1)
                        if t <= (0 if l0 else 1):
                            if l0 or t:
                                pe.wait_ge(out_ok, TG * p + 4)
                        elif l0:
                            pe.wait_ge(zb_lo, TG * p + t)
                        else:
                            pe.wait_ge(zb_lo, TG * p + t - 1)
                        project_x1(t, zb, TA, TAPS).then_inc(zb_mm, 1)
                    if l0:
                        pe.wait_ge(c0_full, TG * i + t + 1)
                        if t:
                            pe.wait_ge(lg_out, TG * i + t)
                        elif shares:
                            pe.wait_ge(mixw_a, 2)
                            pe.wait_ge(mixw_v, 2)
                        for c in range(DC):
                            last = nc.tensor.matmul(ps[:, PR, 0:LG], c0f[:, t, c * P:(c + 1) * P], lgT[:, c, :],
                                                    start=c == 0, stop=c == DC - 1)
                        last.then_inc(lg_mm, 1)
            def phase2(i, l0, l1):
                p = i - 1
                if l0:
                    pe.wait_ge(c0_lo, TG * i + 1)
                    base(0)
                    if not l1:
                        pe.wait_ge(prep_ok, N2 - 2)
                if l1:
                    if l0:
                        pe.wait_ge(lg_out, TG * (i + 1))
                    for ready, taps in ((za_lo, range(TA)), (zb_lo, range(TA, TAPS))):
                        pe.wait_ge(ready, TG * i)
                        last = hi_lo(ps[:, PR, 0:TG * PJ], [(tap_h[:, k, :], tap_l[:, k, :]) for k in taps],
                                     [(zh[:, :, k, :], zl[:, :, k, :]) for k in taps],
                                     start=ready is za_lo, stop=ready is zb_lo)
                    last.then_inc(pj_mm, 1)
                    if not l0:
                        keep_busy(TP0, 28)
                if l0:
                    pe.wait_ge(c0_lo, TG * i + 2)
                    base(1)
                    if not l1:
                        late_step("pj_sum")
                    pe.wait_ge(lw_ok, i + 1)
                    for t in range(TG):
                        last = nc.tensor.transpose(ps[:, TP0, t * P:(t + 1) * P], lw[:, t, :], ident[:, :])
                    last.then_inc(lwT_mm, 1)
                    if not l1:
                        prep(N2)
                        prep(N2 + 1)
                    pe.wait_ge(c0_lo, TG * i + 3)
                    base(2)
                    if not l1:
                        prep(N2 + 2)
                        prep(N2 + 3)
                    pe.wait_ge(lwT_lo, i + 1)
                    for t in range(TG - 1):
                        experts0(t)
                if l1:
                    pe.wait_ge(mw_ok, i)
                    for q in range(TG // 2):
                        last = nc.tensor.transpose(ps[:, TP1, q * P:(q + 1) * P],
                                                   mw[:, 2 * q:2 * q + 2, :].rearrange("p a e -> p (a e)"), ident[:, :])
                    last.then_inc(mwT_mm, 1)
                    if not l0:
                        keep_busy(TP0, 10)
                if l0:
                    pe.wait_ge(c0_lo, TG * i + 4)
                    pe.wait_ge(x1_ok, TG * i + 1)
                    base(3)
                if l1:
                    for t in range(2):
                        pe.wait_ge(mwT_lo, 2 * p + t + 1)
                        experts1(t, d_bank(t, l0))
                if l0:
                    transpose_x1(0)
                    experts0(3)
                if l1:
                    for t in (2, 3):
                        if l0:
                            pe.wait_ge(out_ok, TG * i + t - 1)
                        experts1(t, d_bank(t, l0))

            phase1(0, True, False, shares)
            pe.wait_ge(prep_ok, N2 - 4)
            phase2(0, True, False)
            pe.wait_ge(prep_ok, N1)
            pe.wait_ge(sum_ok, 3)
            with nc.tensor.Fori(1, G) as i:
                phase1(i, True, True)
                phase2(i, True, True)
            phase1(G, False, True)
            phase2(G, False, True)


_INS = ["x", "cond_128", "fside_S_0", "L0_cond_W0", "L0_cond_b0", "L0_cond_W1", "L0_cond_b1", "L0_cond_W2",
        "L0_cond_b2", "L0_cond_weight", "L0_cond_bias_k", "L0_ffn_gate_w", "L0_ffn_base_w", "L0_ffn_base_b",
        "L0_ffn_lora_A", "L0_ffn_lora_B", "L1_cond_weight", "L1_cond_c_weight", "L1_ffn_router_w",
        "L1_ffn_A", "L1_ffn_B"]
_OUTS = [((64, 32, 512), "float32")]


def kernel(**inputs):
    import numpy as _np
    import concourse.bacc as _bacc
    from concourse import mybir as _mybir
    from concourse.bass_utils import run_bass_kernel_spmd as _run

    nc = _bacc.Bacc("TRN2", target_bir_lowering=False, num_devices=1)
    arrays, args = {}, []
    for name in _INS:
        a = _np.ascontiguousarray(inputs[name])
        arrays[f"in_{name}_dram"] = a
        args.append(nc.dram_tensor(f"in_{name}_dram", a.shape, _mybir.dt.from_np(a.dtype), kind="ExternalInput").ap())
    for i, (shape, dtype) in enumerate(_OUTS):
        dt = _mybir.dt.from_np(_np.dtype(dtype))
        args.append(nc.dram_tensor(f"out_{i}_dram", shape, dt, kind="ExternalOutput").ap())
    two_layer_mixer(nc, *args)
    r = _run(nc, [arrays], core_ids=[0])
    return r.results[0]["out_0_dram"]
```

```python
from contextlib import ExitStack

import concourse.bass as bass
from concourse import mybir

F32 = mybir.dt.float32
F32R = mybir.dt.float32r
ALU = mybir.AluOpType
ACT = mybir.ActivationFunctionType
AX_X = mybir.AxisListType.X


def two_layer_mixer(nc: bass.Bass, x, cond, fside, W0, b0, W1, b1, W2, b2, mix_w, mix_b,
                    gate_w, base_w, base_b, lora_A, lora_B, conv_w, ctx_w, router_w, A1, B1, out):
    P = 128
    NB, C, D = x.shape
    TT = NB * C // P
    BT = P // C
    TG = 4
    G = TT // TG
    DC = D // P
    CD = cond.shape[1]
    K0 = W2.shape[1]
    E0, R, _ = lora_A.shape
    ER0 = E0 * R
    LG = ER0 + E0
    E1 = router_w.shape[0]
    ER1 = E1 * R
    PJ = ER1 + E1
    CI, TAPS = conv_w.shape[1:]
    PAD = TAPS // 2
    TA = 5
    TB = TAPS - TA
    SCALE0 = 32.0 / 16.0
    SCALE1 = 16.0 / 16.0 ** 0.5
    assert ER0 == P and 2 * ER1 == P and TA * PJ <= 512 and TG * PJ <= 512 and D == 512

    x_h = x.rearrange("(g t b) c d -> g t (b c) d", g=G, b=BT)
    out_h = out.rearrange("(g t b) c d -> g t (b c) d", g=G, b=BT)

    with ExitStack() as ctx:
        def sb(name, shape, dt=F32):
            return ctx.enter_context(nc.sbuf_tensor(name, shape, dt))

        def sem(name):
            return ctx.enter_context(nc.semaphore(name))

        ident = sb("ident", [P, P])
        ones = sb("ones", [P, P])
        ones_r = sb("ones_r", [P, P], F32R)
        lower = sb("lower", [P, E0, E0])
        same_group = sb("same_group", [P, P // CI])
        x1 = sb("x1", [P, TG, D])
        x1p = sb("x1p", [P, TG, D])
        outb = sb("outb", [P, TG, D])
        cond_s = sb("cond_s", [NB, CD])
        w0_s = sb("w0_s", [P, P])
        w1_s = sb("w1_s", [P, P])
        w2_s = sb("w2_s", [P, K0])
        b0_s = sb("b0_s", [P, 1])
        b1_s = sb("b1_s", [P, 1])
        b2_s = sb("b2_s", [1, K0])
        mixw_s = x1[0:K0, 0:C * C // D, :].rearrange("k t d -> k (t d)")
        mixb_s = sb("mixb_s", [K0, BT, C])
        base_s = sb("base_s", [P, DC, D])
        baseb_s = sb("baseb_s", [P, D])
        la_s = sb("la_s", [P, D])
        gw_s = sb("gw_s", [E0, D])
        lb_in = x1p[:, 0, :].rearrange("p (e o) -> p e o", e=E0)
        b1e_in = x1p[:, 1, 0:E1 * DC * R].rearrange("p (e o) -> p e o", e=E1)
        lb_s = sb("lb_s", [P, DC, E0, R])
        conv_s = sb("conv_s", [P, CI, TAPS])
        ctxw_s = sb("ctxw_s", [P, CD])
        fside_s = sb("fside_s", [P, 1])
        a1_s = sb("a1_s", [PJ, D])
        b1e_s = sb("b1e_s", [P, DC, 2, E1, R])
        warm = sb("warm", [P, 1])
        condT = sb("condT", [P, NB])
        ctxwT = sb("ctxwT", [P, P])
        h1T = sb("h1T", [P, NB])
        h2T = sb("h2T", [P, NB])
        att_m = sb("att_m", [NB, 1])
        att_e = sb("att_e", [NB, K0])
        att_s = sb("att_s", [NB, 1])
        att_r = sb("att_r", [NB, 1])
        att3 = sb("att3", [NB, 3, 32])
        att3T = sb("att3T", [P, NB], F32R)
        attT = sb("attT", [K0, NB])
        mixT = sb("mixT", [P, TT, P])
        mixbias = sb("mixbias", [P, TT])
        ctxbias = sb("ctxbias", [P, TT])
        lgT = sb("lgT", [P, DC, LG])
        lg_c = sb("lg_c", [P, LG])
        lg_sum = sb("lg_sum", [P, LG])
        base_sum = sb("base_sum", [P, D])
        pj_c = sb("pj_c", [P, PJ])
        pj_sum = sb("pj_sum", [P, PJ])
        base_rows = sb("base_rows", [P, DC])
        a1T = sb("a1T", [P, 2, DC, PJ], F32R)
        a1_pad = sb("a1_pad", [PAD, 2, PJ])
        a1_rows = nc.dram_tensor("a1_rows", [2, PAD + D + PAD, PJ], F32, kind="Internal").ap()
        base_h = sb("base_h", [P, DC, D], F32R)
        base_l = sb("base_l", [P, DC, D], F32R)
        lb_h = sb("lb_h", [P, D], F32R)
        lb_l = sb("lb_l", [P, D], F32R)
        pj_h = sb("pj_h", [P, DC, TAPS, PJ], F32R)
        pj_l = sb("pj_l", [P, DC, TAPS, PJ], F32R)
        tapm = outb[:, :, :].rearrange("p t d -> p (t d)")[:, 0:TAPS * P].rearrange("p (k c) -> p k c", c=P)
        tap_h = sb("tap_h", [P, TAPS, P], F32R)
        tap_l = sb("tap_l", [P, TAPS, P], F32R)
        b1e_h = sb("b1e_h", [P, D], F32R)
        b1e_l = sb("b1e_l", [P, D], F32R)
        xr = sb("xr", [P, TG, D])
        xb = sb("xb", [P, TG, D])
        c0f = sb("c0f", [P, TG, D])
        c0h = sb("c0h", [P, TG, D], F32R)
        c0l = sb("c0l", [P, TG, D], F32R)
        lgs = sb("lgs", [P, TG, LG])
        lw = sb("lw", [P, TG, ER0])
        lwTh = sb("lwTh", [P, TG * P], F32R)
        lwTl = sb("lwTl", [P, TG * P], F32R)
        x1Th = sb("x1Th", [P, 2, D], F32R)
        x1Tl = sb("x1Tl", [P, 2, D], F32R)
        zh = sb("zh", [P, TG, TAPS, PJ], F32R)
        zl = sb("zl", [P, TG, TAPS, PJ], F32R)
        mixw3 = zh[:, :, :, :].rearrange("p t k e -> p (t k e)")[:, 0:C * C]
        pj_ctx = sb("pj_ctx", [P, TG, PJ])
        pj = sb("pj", [P, TG, PJ])
        mw = sb("mw", [P, TG, ER1])
        mwT = sb("mwT", [P, TG * P], F32R)

        def gate_tiles(n, e):
            return dict(top=sb(f"top{n}", [P, TG]), above=sb(f"above{n}", [P, TG, e, 2, e]),
                        eq=sb(f"eq{n}", [P, TG, e, e]), rank=sb(f"rank{n}", [P, TG, e]),
                        dif=sb(f"dif{n}", [P, TG, e]), ex=sb(f"ex{n}", [P, TG, e]),
                        kept=sb(f"kept{n}", [P, TG, e]), tot=sb(f"tot{n}", [P, TG]),
                        inv=sb(f"inv{n}", [P, TG]), w=sb(f"w{n}", [P, TG, e]))

        gate0 = gate_tiles(0, E0)
        gate1 = gate_tiles(1, E1)

        ps = ctx.enter_context(nc.psum_tensor("ps", [P, 8, 512], F32))
        TP0, TP1, ZA, ZB, PR, Y = 0, 1, 2, 3, 4, 5
        MISC = 3
        y_bank = [Y, Y + 1, Y + 2, Y]

        def z_banks(t, l0):
            return (ZA, ZB) if l0 or t % 2 else (Y, Y + 1)

        def c0_bank(t, l1):
            return TP0 if l1 else t % 2

        def d_bank(t, l0):
            return ZA + t % 2 if l0 else ZA + t if t < 2 else Y + t - 2

        consts = sem("consts")
        const_step = sem("const_step")
        in_cond, in_w0, in_b0, in_w1, in_b1, in_w2, in_b2, in_mixw, in_mixb = (
            sem(f"in_{n}") for n in ("cond", "w0", "b0", "w1", "b1", "w2", "b2", "mixw", "mixb"))
        in_base = [sem(f"in_base{c}") for c in range(DC)]
        in_lg, in_baseb, in_lb, in_conv, in_ctx, in_fside, in_a1, in_b1e = (
            sem(f"in_{n}") for n in ("lg", "baseb", "lb", "conv", "ctx", "fside", "a1", "b1e"))
        x_in = [sem(f"x_in{t}") for t in range(TG)]
        out_done = [sem(f"out_done{t}") for t in range(TG)]
        condT_mm, condT_ok, h1_mm, h1_ok, h2_mm, h2_ok, att_mm = (
            sem(n) for n in ("condT_mm", "condT_ok", "h1_mm", "h1_ok", "h2_mm", "h2_ok", "att_mm"))
        att_max, att_exp, att_inv, att_ok, att3_zero, attT_mm, att3_hi, att3_ok, attT_ok = (
            sem(n) for n in ("att_max", "att_exp", "att_inv", "att_ok", "att3_zero", "attT_mm",
                             "att3_hi", "att3_ok", "attT_ok"))
        mixw3_zero, mixw3_hi, mixw3_ok, warm_ok, lgT_mm, lg_ok = (
            sem(n) for n in ("mixw3_zero", "mixw3_hi", "mixw3_ok", "warm_ok", "lgT_mm", "lg_ok"))
        mixb_mm, mixb_ok, ctx_mm, ctx_ok, mixw_mm, mixw_a, mixw_v = (
            sem(n) for n in ("mixb_mm", "mixb_ok", "ctx_mm", "ctx_ok", "mixw_mm", "mixw_a", "mixw_v"))
        sum_mm, sum_ok, mix_zero, tap_ok, pad_ok = (
            sem(n) for n in ("sum_mm", "sum_ok", "mix_zero", "tap_ok", "pad_ok"))
        half_ok = sem("half_ok")
        inner_ok, a1_out, in_pj, lgc_ok, pjc_ok, rows_ok, diag_ok = (
            sem(n) for n in ("inner_ok", "a1_out", "in_pj", "lgc_ok", "pjc_ok", "rows_ok", "diag_ok"))
        prep_mm, prep_hi, prep_ok = sem("prep_mm"), sem("prep_hi"), sem("prep_ok")
        c0_mm, c0_full, c0_hi, c0_lo, lg_mm, lg_out = (
            sem(n) for n in ("c0_mm", "c0_full", "c0_hi", "c0_lo", "lg_mm", "lg_out"))
        gate0_step, dif0_ok, ex0_ok, lw_ok, lwT_mm, lwT_hi, lwT_lo = (
            sem(n) for n in ("gate0_step", "dif0_ok", "ex0_ok", "lw_ok", "lwT_mm", "lwT_hi", "lwT_lo"))
        bias_ok, xb_step, xb_ok, y_mm, x1_ok, x1p_ok, pj_ctx_ok = (
            sem(n) for n in ("bias_ok", "xb_step", "xb_ok", "y_mm", "x1_ok", "x1p_ok", "pj_ctx_ok"))
        x1T_mm, x1T_hi, x1T_lo, za_mm, za_hi, za_lo, zb_mm, zb_hi, zb_lo = (
            sem(n) for n in ("x1T_mm", "x1T_hi", "x1T_lo", "za_mm", "za_hi", "za_lo",
                             "zb_mm", "zb_hi", "zb_lo"))
        pj_mm, pj_ok, gate1_step, dif1_ok, ex1_ok, mw_ok, mwT_mm, mwT_hi, mwT_lo, d_mm, out_ok = (
            sem(n) for n in ("pj_mm", "pj_ok", "gate1_step", "dif1_ok", "ex1_ok", "mw_ok",
                             "mwT_mm", "mwT_hi", "mwT_lo", "d_mm", "out_ok"))

        base_diag = x1[:, TG - 1, :].rearrange("p (o q) -> p o q", q=P)

        def lg_unit(c0):
            moves = []
            for n, c in enumerate((c0, c0 + 1)):
                moves.append((n * LG, la_s[:, c * P:(c + 1) * P]))
                moves.append((n * LG + ER0, gw_s[:, c * P:(c + 1) * P]))
            return dict(need=[(in_lg, 32)], moves=moves, n=2 * LG,
                        full=lgT[:, c0:c0 + 2, :].rearrange("p c e -> p (c e)"))

        def base_unit(c):
            return dict(need=[(in_base[c], 16)], n=D, hi=base_h[:, c, :], lo=base_l[:, c, :],
                        moves=[(o * P, base_s[:, o, c * P:(c + 1) * P]) for o in range(DC)])

        def ctxw_unit():
            return dict(need=[(in_ctx, 16)], moves=[(0, ctxw_s[:, :])], full=ctxwT[:, :], n=P)

        def lb_unit():
            return dict(need=[(inner_ok, 1)], n=D, hi=lb_h[:, :], lo=lb_l[:, :], spread=DC,
                        moves=[(o * P, lb_s[:, o, :, :].rearrange("p e r -> p (e r)")) for o in range(DC)])

        def a1_unit():
            return dict(need=[(in_a1, 32)], n=DC * PJ, hi=a1T[:, 0, :, :].rearrange("p c e -> p (c e)"),
                        lo=a1T[:, 1, :, :].rearrange("p c e -> p (c e)"),
                        moves=[(c * PJ, a1_s[:, c * P:(c + 1) * P]) for c in range(DC)])

        def tap_unit(k0, k1):
            return dict(need=[(tap_ok, TAPS)], n=(k1 - k0) * P,
                        hi=tap_h[:, k0:k1, :].rearrange("p k e -> p (k e)"),
                        lo=tap_l[:, k0:k1, :].rearrange("p k e -> p (k e)"),
                        moves=[((k - k0) * P, tapm[:, k, :]) for k in range(k0, k1)])

        def b1e_unit():
            return dict(need=[(inner_ok, 3)], n=D, hi=b1e_h[:, :], lo=b1e_l[:, :], spread=DC,
                        moves=[(o * P, b1e_s[:, o, :, :, :].rearrange("p a e r -> p (a e r)"))
                               for o in range(DC)])

        lg_units = [lg_unit(0), lg_unit(2)]
        for u, bank in zip(lg_units, (TP0, ZA)):
            u["bank"], u["src"] = bank, ps[:, bank, 0:u["n"]]
        units = [a1_unit()] + [base_unit(c) for c in range(DC)] + [ctxw_unit(), lb_unit()]
        N2 = len(units)
        units += [tap_unit(k, k + 3) for k in range(0, TAPS, 3)] + [b1e_unit()]
        N1 = len(units)
        PREP_BANKS = (ZA, Y, Y + 1, Y + 2, ZA, Y, Y + 1, TP1, ZA, TP1, ZA)
        for n, u in enumerate(units):
            u["bank"] = PREP_BANKS[n]
            before = [m for m in range(n) if units[m]["bank"] == u["bank"]]
            u["after"] = before[-1] + 1 if before else 0
            u["his"] = sum("hi" in v for v in units[:n + 1])
            u["src"] = ps[:, u["bank"], 0:u["n"]]
            if "spread" in u:
                u["src"] = u["src"].rearrange("p (o q) -> p q o", o=u["spread"])
                u["hi"], u["lo"] = (v.rearrange("p (q o) -> p q o", o=u["spread"]) for v in (u["hi"], u["lo"]))
        assert N2 == 7 and N1 == len(PREP_BANKS)
        shares = [[0, 1, 2, "lg_sum"], [3, "base_rows"], [4, 5, "pj_c", "base_rows"], [6, "base_rows"]]
        FIRST = 2

        def copy_mix_blocks(copy, quads, tiles):
            for q in quads:
                for j in range(BT):
                    src = ps[q * C:(q + 1) * C, PR, :].rearrange("p (m n) -> p m n", n=NB)[:, :, j:NB:BT][:, :, tiles]
                    last = copy(mixT[j * C:(j + 1) * C, tiles, j * C + q:(j + 1) * C:BT], src.rearrange("p m n -> p n m"))
            return last

        def mw_half(where, half, a):
            rows = slice(half * ER1, (half + 1) * ER1)
            if where is ps:
                return ps[rows, TP1, 0:TG // 2 * P].rearrange("p (q n) -> p q n", n=P)
            return mwT[rows, :].rearrange("p (q a n) -> p q a n", a=2, n=P)[:, :, a, :]

        block = ctx.enter_context(nc.Block())

        @block.sync
        def _(sp):
            def load_x(g, t):
                sp.dma_start(xr[:, t, :], x_h[g, t]).then_inc(x_in[t], 16)

            def refill(g):
                for t in range(TG):
                    sp.wait_ge(c0_mm, TG * (g - 1) + t + 1)
                    sp.wait_ge(xb_ok, TG * (g - 1) + t + 1)
                    load_x(g, t)

            def store(g, tiles=range(TG)):
                for t in tiles:
                    sp.wait_ge(out_ok, TG * (g + 1) + t + 1)
                    sp.dma_start(out_h[g, t], outb[:, t, :]).then_inc(out_done[t], 16)

            sp.dma_start(cond_s[:, :], cond).then_inc(in_cond, 16)
            sp.dma_start(w0_s[:, :], W0).then_inc(in_w0, 16)
            sp.dma_start(b0_s[:, :], b0.rearrange("(p a) -> p a", a=1)).then_inc(in_b0, 16)
            sp.dma_start(mixw_s[:, :], mix_w.rearrange("k o i a -> k (o i a)")).then_inc(in_mixw, 16)
            sp.dma_start(w1_s[:, :], W1).then_inc(in_w1, 16)
            sp.dma_start(b1_s[:, :], b1.rearrange("(p a) -> p a", a=1)).then_inc(in_b1, 16)
            sp.dma_start(w2_s[:, :], W2).then_inc(in_w2, 16)
            sp.dma_start(b2_s[:, :], b2.rearrange("(a k) -> a k", a=1)).then_inc(in_b2, 16)
            sp.dma_start(la_s[:, :], lora_A.rearrange("e r d -> (e r) d")).then_inc(in_lg, 16)
            sp.dma_start(gw_s[:, :], gate_w).then_inc(in_lg, 16)
            sp.dma_start(a1_s[0:ER1, :], A1.rearrange("e r d -> (e r) d")).then_inc(in_a1, 16)
            sp.dma_start(a1_s[ER1:PJ, :], router_w).then_inc(in_a1, 16)
            load_x(0, 0)
            sp.dma_start(mixb_s[:, :, :], mix_b.unsqueeze(1).to_broadcast([K0, BT, C])).then_inc(in_mixb, 16)
            for c in range(DC):
                sp.dma_start(base_s[:, :, c * P:(c + 1) * P],
                             base_w.rearrange("(o p) d -> p o d", p=P)[:, :, c * P:(c + 1) * P]).then_inc(in_base[c], 16)
                if c == 1:
                    load_x(0, 1)
            sp.dma_start(ctxw_s[:, :], ctx_w.partition_broadcast(BT)).then_inc(in_ctx, 16)
            load_x(0, 2)
            sp.dma_start(lb_in, lora_B.rearrange("e (p o) r -> p e (o r)", p=P)).then_inc(in_lb, 16)
            load_x(0, 3)
            sp.dma_start(conv_s[:, :, :], conv_w.partition_broadcast(BT)).then_inc(in_conv, 16)
            sp.dma_start(fside_s[:, :], fside.rearrange("(p a) -> p a", a=1).partition_broadcast(BT)).then_inc(in_fside, 16)
            sp.dma_start(b1e_in, B1.rearrange("e (p o) r -> p e (o r)", p=P)).then_inc(in_b1e, 16)
            sp.wait_ge(pad_ok, 1)
            for row in (0, PAD + D):
                sp.dma_start(a1_rows[:, row:row + PAD, :].rearrange("h r e -> r h e"), a1_pad[:, :, :]).then_inc(a1_out, 16)
            sp.wait_ge(prep_ok, 1)
            for h in range(2):
                sp.dma_start(a1_rows[h, PAD:PAD + D, :].rearrange("(c p) e -> p c e", p=P),
                             a1T[:, h, :, :].bitcast(F32)).then_inc(a1_out, 16)
            sp.wait_ge(a1_out, 64)
            for h, part in enumerate((pj_h, pj_l)):
                shifted = bass.AP(a1_rows.tensor, h * (D + 2 * PAD) * PJ, [[PJ, P], [P * PJ, DC], [1, TAPS * PJ]])
                sp.dma_start(part[:, :, :, :].bitcast(F32).rearrange("p c k e -> p c (k e)"), shifted).then_inc(in_pj, 16)
            for t in range(TG):
                sp.sem_inc(out_done[t], 16)
            refill(1)
            with nc.sync.Fori(1, G - 1) as i:
                refill(i + 1)
                store(i - 1)
            store(G - 2)
            for half, ready, count in ((slice(0, D // 2), half_ok, 1), (slice(D // 2, D), out_ok, TG * G + 1)):
                sp.wait_ge(ready, count)
                sp.dma_start(out_h[G - 1, 0][:, half], outb[:, 0, half]).then_inc(out_done[0], 16)
            store(G - 1, range(1, TG))
            for t in range(TG):
                sp.wait_ge(out_done[t], 16 * (G + 1 + (t == 0)))

        @block.gpsimd
        def _(pool):
            nc.gpsimd.memset(warm[:, :], 0.0).then_inc(warm_ok, 1)
            nc.gpsimd.memset(ident[:, :], 0.0).then_inc(const_step, 1)
            pool.wait_ge(const_step, 1)
            nc.gpsimd.affine_select(out=ident[:, :], in_=ident[:, :], compare_op=ALU.not_equal, fill=1.0,
                                    base=0, pattern=[[-1, P]], channel_multiplier=1).then_inc(consts, 1)
            nc.gpsimd.memset(ones[:, :], 1.0).then_inc(consts, 1)
            nc.gpsimd.memset(ones_r[:, :].bitcast(F32), 1.0).then_inc(consts, 1)
            nc.gpsimd.memset(mixw3.bitcast(F32), 0.0).then_inc(mixw3_zero, 1)
            nc.gpsimd.memset(att3[:, :, :], 0.0).then_inc(att3_zero, 1)
            nc.gpsimd.memset(mixT[:, :, :], 0.0).then_inc(mix_zero, 1)
            nc.gpsimd.memset(lower[:, :, :], 1.0).then_inc(const_step, 1)
            pool.wait_ge(const_step, 2)
            nc.gpsimd.affine_select(out=lower[:, :, :], in_=lower[:, :, :], compare_op=ALU.is_gt, fill=0.0,
                                    base=0, pattern=[[1, E0], [-1, E0]], channel_multiplier=0).then_inc(consts, 1)
            nc.gpsimd.memset(a1_pad[:, :, :], 0.0).then_inc(pad_ok, 1)
            nc.gpsimd.memset(same_group[:, :], 1.0).then_inc(const_step, 1)
            pool.wait_ge(const_step, 3)
            nc.gpsimd.affine_select(out=same_group[:, :], in_=same_group[:, :], compare_op=ALU.is_ge, fill=0.0,
                                    base=0, pattern=[[-CI, P // CI]], channel_multiplier=1).then_inc(const_step, 1)
            pool.wait_ge(const_step, 4)
            nc.gpsimd.affine_select(out=same_group[:, :], in_=same_group[:, :], compare_op=ALU.is_ge, fill=0.0,
                                    base=CI - 1, pattern=[[CI, P // CI]], channel_multiplier=-1).then_inc(const_step, 1)
            pool.wait_ge(in_lb, 16)
            nc.gpsimd.tensor_copy(lb_s[:, :, :, :], lb_in.rearrange("p e (o r) -> p o e r", r=R)).then_inc(inner_ok, 1)
            pool.wait_ge(const_step, 5)
            pool.dma_start(baseb_s[:, :], base_b.partition_broadcast(P)).then_inc(in_baseb, 16)
            pool.wait_ge(in_conv, 16)
            for k in range(TAPS):
                nc.gpsimd.tensor_tensor(tapm[:, k, :].rearrange("p (g c) -> p g c", c=CI),
                                        conv_s[:, :, TAPS - 1 - k].unsqueeze(1).to_broadcast([P, P // CI, CI]),
                                        same_group[:, :].unsqueeze(2).to_broadcast([P, P // CI, CI]),
                                        ALU.mult).then_inc(tap_ok, 1)

            pool.wait_ge(consts, 1)
            pool.wait_ge(rows_ok, DC)
            nc.gpsimd.tensor_tensor(base_diag, ident[:, :].unsqueeze(1).to_broadcast([P, DC, P]),
                                    base_rows[:, :].unsqueeze(2).to_broadcast([P, DC, P]), ALU.mult).then_inc(diag_ok, 1)
            pool.wait_ge(in_b1e, 16)
            for n in range(2):
                nc.gpsimd.tensor_copy(b1e_s[:, :, n, :, :],
                                      b1e_in.rearrange("p e (o r) -> p o e r", r=R)).then_inc(inner_ok, 1)

            def bias_x(i, t):
                pool.wait_ge(x_in[t], 16 * (i + 1))
                pool.wait_ge(bias_ok, TG * i + t + 1)
                nc.gpsimd.tensor_tensor(xb[:, t, :], xb[:, t, :], xr[:, t, :], ALU.add).then_inc(xb_step, 1)
                pool.wait_ge(xb_step, TG * i + t + 1)
                nc.gpsimd.tensor_tensor(xb[:, t, :], xb[:, t, :], baseb_s[:, :], ALU.add).then_inc(xb_ok, 1)

            def context(p, after):
                if after:
                    pool.wait_ge(pj_ok, p)
                nc.gpsimd.tensor_tensor(pj_ctx[:, :, :], pj_sum[:, :].unsqueeze(1).to_broadcast([P, TG, PJ]),
                                        ctxbias[:, bass.ds(TG * p, TG)].unsqueeze(2).to_broadcast([P, TG, PJ]),
                                        ALU.mult).then_inc(pj_ctx_ok, 1)

            pool.wait_ge(in_baseb, 16)
            for t in range(TG):
                bias_x(0, t)
            pool.wait_ge(sum_ok, 3)
            pool.wait_ge(ctx_ok, 1)
            context(0, False)
            with nc.gpsimd.Fori(1, G) as i:
                for t in range(TG):
                    bias_x(i, t)
                context(i, True)

        @block.scalar
        def _(act):
            def prep(n):
                u = units[n]
                if "hi" in u:
                    act.wait_ge(prep_mm, n + 1)
                    nc.scalar.activation(u["hi"], u["src"], ACT.Copy).then_inc(prep_hi, 1)

            act.wait_ge(warm_ok, 1)
            nc.scalar.activation(warm[:, :], warm[:, :], ACT.Gelu)
            act.wait_ge(in_b0, 16)
            act.wait_ge(h1_mm, 1)
            nc.scalar.activation(h1T[:, :], ps[:, MISC, 0:NB], ACT.Gelu, bias=b0_s[:, :]).then_inc(h1_ok, 1)
            act.wait_ge(in_b1, 16)
            act.wait_ge(h2_mm, 1)
            nc.scalar.activation(h2T[:, :], ps[:, MISC, 0:NB], ACT.Gelu, bias=b1_s[:, :]).then_inc(h2_ok, 1)
            act.wait_ge(att_max, 1)
            nc.scalar.activation(att_e[:, :], ps[0:NB, Y, 0:K0], ACT.Exp, bias=att_m[:, :],
                                 accum_out=att_s[:, :]).then_inc(att_exp, 1)
            for n, u in enumerate(lg_units):
                act.wait_ge(lgT_mm, n + 1)
                nc.scalar.activation(u["full"], u["src"], ACT.Copy).then_inc(lg_ok, 1)
            act.wait_ge(mixw_mm, 1)
            act.wait_ge(mix_zero, 1)
            for tiles in (slice(0, TG), slice(TG, TT)):
                copy_mix_blocks(nc.scalar.copy, (0, 1), tiles).then_inc(mixw_a, 1)

            def late_step(n, t=None):
                if n == "lg_sum":
                    act.wait_ge(sum_mm, 1)
                    nc.scalar.activation(lg_sum[:, :], ps[:, MISC, 0:LG], ACT.Copy).then_inc(sum_ok, 1)
                elif n == "pj_sum":
                    act.wait_ge(sum_mm, 3)
                    nc.scalar.activation(pj_sum[:, :], ps[:, MISC, 0:PJ], ACT.Copy).then_inc(sum_ok, 1)
                elif n == "base_rows":
                    for c in range(DC):
                        act.wait_ge(in_base[c], 16)
                    for o in range(*((t - 1, t) if t < TG - 1 else (t - 1, DC))):
                        nc.scalar.activation(xb[:, o, :], base_s[:, o, :], ACT.Copy,
                                             accum_out=base_rows[:, o:o + 1]).then_inc(rows_ok, 1)
                elif n == "base_sum":
                    act.wait_ge(sum_mm, 2)
                    nc.scalar.activation(base_sum[:, :], ps[:, MISC, 0:D], ACT.Copy).then_inc(sum_ok, 1)
                elif n != "pj_c":
                    prep(n)

            def bias_term(i, t):
                nc.scalar.activation(xb[:, t, :], base_sum[:, :], ACT.Copy,
                                     scale=mixbias[:, bass.ds(TG * i + t, 1)]).then_inc(bias_ok, 1)

            def keep_x1(i, t):
                act.wait_ge(out_ok, TG * (i - 1) + t + 1)
                act.wait_ge(x1_ok, TG * (i - 1) + t + 1)
                nc.scalar.activation(x1p[:, t, :], x1[:, t, :], ACT.Copy).then_inc(x1p_ok, 1)

            def phase1(i, l0, l1, shares=None):
                p = i - 1
                for t in range(TG):
                    if l0:
                        act.wait_ge(c0_mm, TG * i + t + 1)
                        nc.scalar.activation(c0f[:, t, :], ps[:, c0_bank(t, l1), :], ACT.Copy).then_inc(c0_full, 1)
                        nc.scalar.activation(c0h[:, t, :], ps[:, c0_bank(t, l1), :], ACT.Copy).then_inc(c0_hi, 1)
                    for n in (shares[t] if shares else ()):
                        late_step(n, t)
                    if l1:
                        if t + 1 < TG:
                            act.wait_ge(x1T_mm, TG * p + t + 2)
                            nc.scalar.activation(x1Th[:, (t + 1) % 2, :], ps[:, TP1, :], ACT.Copy).then_inc(x1T_hi, 1)
                        za, zb = z_banks(t, l0)
                        act.wait_ge(za_mm, TG * p + t + 1)
                        nc.scalar.activation(zh[:, t, 0:TA, :].rearrange("p k e -> p (k e)"),
                                             ps[:, za, 0:TA * PJ], ACT.Copy).then_inc(za_hi, 1)
                        act.wait_ge(zb_mm, TG * p + t + 1)
                        nc.scalar.activation(zh[:, t, TA:TAPS, :].rearrange("p k e -> p (k e)"),
                                             ps[:, zb, 0:TB * PJ], ACT.Copy).then_inc(zb_hi, 1)
                        keep_x1(i, t)
                        if l0:
                            bias_term(i, t)

            def phase2(i, l0, l1):
                if l0:
                    act.wait_ge(dif0_ok, i + 1)
                    nc.scalar.activation(gate0["ex"][:, :, :], gate0["dif"][:, :, :], ACT.Exp).then_inc(ex0_ok, 1)
                if not l1:
                    late_step("base_sum")
                    act.wait_ge(mixb_ok, 1)
                    act.wait_ge(sum_ok, 2)
                    bias_term(0, 0)
                if l1:
                    act.wait_ge(dif1_ok, i)
                    nc.scalar.activation(gate1["ex"][:, :, :], gate1["dif"][:, :, :], ACT.Exp).then_inc(ex1_ok, 1)
                if l0:
                    act.wait_ge(lwT_mm, i + 1)
                    nc.scalar.activation(lwTh[:, :], ps[:, TP0, :], ACT.Copy).then_inc(lwT_hi, 1)
                if not l1:
                    for n in range(N2, N2 + 2):
                        prep(n)
                    for t in range(1, TG - 1):
                        bias_term(0, t)
                    late_step("pj_sum")
                    for n in range(N2 + 2, N1):
                        prep(n)
                    bias_term(0, TG - 1)
                if l1:
                    act.wait_ge(mwT_mm, i)
                    for a in range(2):
                        nc.scalar.activation(mw_half(mwT, 0, a), mw_half(ps, a, a), ACT.Copy).then_inc(mwT_hi, 1)
                if l0:
                    act.wait_ge(x1T_mm, TG * i + 1)
                    nc.scalar.activation(x1Th[:, 0, :], ps[:, TP1, :], ACT.Copy).then_inc(x1T_hi, 1)

            phase1(0, True, False, shares)
            phase2(0, True, False)
            with nc.scalar.Fori(1, G) as i:
                phase1(i, True, True)
                phase2(i, True, True)
            phase1(G, False, True)
            phase2(G, False, True)

        @block.vector
        def _(dve):
            def prep(n):
                u = units[n]
                if "hi" in u:
                    dve.wait_ge(prep_hi, u["his"])
                    nc.vector.tensor_tensor(u["lo"], u["src"], u["hi"].bitcast(F32), ALU.subtract).then_inc(prep_ok, 1)
                else:
                    dve.wait_ge(prep_mm, n + 1)
                    nc.vector.tensor_copy(u["full"], u["src"]).then_inc(prep_ok, 1)

            dve.wait_ge(condT_mm, 1)
            nc.vector.tensor_copy(condT[:, :], ps[:, MISC, 0:NB]).then_inc(condT_ok, 1)
            dve.wait_ge(in_mixw, 16)
            dve.wait_ge(mixw3_zero, 1)
            for n in range(2):
                nc.vector.tensor_copy(mixw3[32 * n:32 * n + K0, :], mixw_s).then_inc(mixw3_hi, 1)
            dve.wait_ge(mixw3_hi, 1)
            nc.vector.tensor_tensor(mixw3[64:64 + K0, :], mixw_s, mixw3[0:K0, :].bitcast(F32),
                                    ALU.subtract).then_inc(mixw3_ok, 1)
            dve.wait_ge(att_mm, 1)
            nc.vector.reduce_max(att_m[:, :], ps[0:NB, Y, 0:K0], AX_X, negate=True).then_inc(att_max, 1)
            dve.wait_ge(att_exp, 1)
            nc.vector.reciprocal(att_r[:, :], att_s[:, :]).then_inc(att_inv, 1)
            dve.wait_ge(att_inv, 1)
            dve.wait_ge(att3_zero, 1)
            nc.vector.tensor_scalar(att3[:, :, 0:K0], att_e[:, :].unsqueeze(1).to_broadcast([NB, 3, K0]),
                                    att_r[:, 0:1], None, ALU.mult).then_inc(att_ok, 1)
            dve.wait_ge(attT_mm, 1)
            nc.vector.tensor_copy(att3T[0:64 + K0, :], ps[0:64 + K0, MISC, 0:NB]).then_inc(att3_hi, 1)
            dve.wait_ge(att3_hi, 1)
            nc.vector.tensor_tensor(att3T[32:32 + K0, :], ps[32:32 + K0, MISC, 0:NB],
                                    att3T[32:32 + K0, :].bitcast(F32), ALU.subtract).then_inc(att3_ok, 1)
            nc.vector.tensor_copy(attT[:, :], ps[0:K0, MISC, 0:NB]).then_inc(attT_ok, 1)
            dve.wait_ge(lg_ok, 2)
            nc.vector.reduce_sum(lg_c[:, :], lgT[:, :, :].rearrange("p c e -> p e c"), AX_X).then_inc(lgc_ok, 1)
            dve.wait_ge(mixw_mm, 1)
            dve.wait_ge(mix_zero, 1)
            for tiles in (slice(0, TG), slice(TG, TT)):
                copy_mix_blocks(nc.vector.tensor_copy, (2, 3), tiles).then_inc(mixw_v, 1)
            dve.wait_ge(mixb_mm, 1)
            for j in range(BT):
                last = nc.vector.tensor_copy(mixbias[j * C:(j + 1) * C, :], ps[j * C:(j + 1) * C, MISC, j:NB:BT])
            last.then_inc(mixb_ok, 1)
            dve.wait_ge(consts, 4)
            dve.wait_ge(mixb_ok, 1)

            def gates(i, g, logits, e, scale, step_sem, dif_ok, ex_ok, n0, out_w):
                count = [0]

                def step(ins):
                    count[0] += 1
                    ins.then_inc(step_sem, 1)
                    dve.wait_ge(step_sem, n0 + count[0])

                per_f = logits.unsqueeze(2).to_broadcast([P, TG, e, e])
                per_e = logits.unsqueeze(3).to_broadcast([P, TG, e, e])
                above = g["above"]
                nc.vector.reduce_max(g["top"][:, :], logits, AX_X)
                nc.vector.tensor_tensor(g["eq"][:, :, :, :], per_f, per_e, ALU.is_equal)
                step(nc.vector.tensor_tensor(above[:, :, :, 0, :], per_f, per_e, ALU.is_gt))
                nc.vector.tensor_tensor(g["dif"][:, :, :], logits,
                                        g["top"][:, :].unsqueeze(2).to_broadcast([P, TG, e]),
                                        ALU.subtract).then_inc(dif_ok, 1)
                low = lower[:, 0:e, 0:e].unsqueeze(1).to_broadcast([P, TG, e, e])
                step(nc.vector.tensor_tensor(above[:, :, :, 1, :], g["eq"][:, :, :, :], low, ALU.mult))
                step(nc.vector.reduce_sum(g["rank"][:, :, :], above[:, :, :, :, :].rearrange("p t e a f -> p t e (a f)"), AX_X))
                dve.wait_ge(ex_ok, i)
                step(nc.vector.scalar_tensor_tensor(out=g["kept"][:, :, :], in0=g["rank"][:, :, :], scalar=2.0,
                                                    in1=g["ex"][:, :, :], op0=ALU.is_lt, op1=ALU.mult))
                step(nc.vector.reduce_sum(g["tot"][:, :], g["kept"][:, :, :], AX_X))
                step(nc.vector.reciprocal(g["inv"][:, :], g["tot"][:, :]))
                step(nc.vector.scalar_tensor_tensor(out=g["w"][:, :, :], in0=g["kept"][:, :, :], scalar=scale,
                                                    in1=g["inv"][:, :].unsqueeze(2).to_broadcast([P, TG, e]),
                                                    op0=ALU.mult, op1=ALU.mult))
                assert count[0] == GATE_STEPS

            GATE_STEPS = 7

            def minus_hi(lo, bank, hi):
                return nc.vector.tensor_tensor(lo, bank, hi.bitcast(F32), ALU.subtract)

            def late_step(n):
                if n == "ctx":
                    dve.wait_ge(ctx_mm, 1)
                    dve.wait_ge(in_fside, 16)
                    for j in range(BT):
                        rows = slice(j * C, (j + 1) * C)
                        last = nc.vector.tensor_scalar(ctxbias[rows, :], ps[rows, PR, j:NB:BT],
                                                       fside_s[rows, 0:1], None, ALU.add)
                    last.then_inc(ctx_ok, 1)
                elif n == "pj_c":
                    dve.wait_ge(prep_ok, 1)
                    nc.vector.reduce_sum(pj_c[:, :], a1T[:, :, :, :].bitcast(F32).rearrange("p h c e -> p e (h c)"),
                                         AX_X).then_inc(pjc_ok, 1)
                elif n not in ("base_rows", "lg_sum"):
                    prep(n)

            def phase1(i, l0, l1, shares=None):
                p = i - 1
                for t in range(TG):
                    if l0:
                        dve.wait_ge(c0_hi, TG * i + t + 1)
                        minus_hi(c0l[:, t, :], c0f[:, t, :], c0h[:, t, :]).then_inc(c0_lo, 1)
                    if l1:
                        if t + 1 < TG:
                            dve.wait_ge(x1T_hi, TG * p + t + 2)
                            minus_hi(x1Tl[:, (t + 1) % 2, :], ps[:, TP1, :], x1Th[:, (t + 1) % 2, :]).then_inc(x1T_lo, 1)
                        za, zb = z_banks(t, l0)
                        dve.wait_ge(za_hi, TG * p + t + 1)
                        minus_hi(zl[:, t, 0:TA, :].rearrange("p k e -> p (k e)"), ps[:, za, 0:TA * PJ],
                                 zh[:, t, 0:TA, :].rearrange("p k e -> p (k e)")).then_inc(za_lo, 1)
                        dve.wait_ge(zb_hi, TG * p + t + 1)
                        minus_hi(zl[:, t, TA:TAPS, :].rearrange("p k e -> p (k e)"), ps[:, zb, 0:TB * PJ],
                                 zh[:, t, TA:TAPS, :].rearrange("p k e -> p (k e)")).then_inc(zb_lo, 1)
                    if l0:
                        dve.wait_ge(lg_mm, TG * i + t + 1)
                        if shares and t == 0:
                            dve.wait_ge(sum_ok, 1)
                        nc.vector.scalar_tensor_tensor(out=lgs[:, t, :], in0=lg_sum[:, :],
                                                       scalar=mixbias[:, bass.ds(TG * i + t, 1)],
                                                       in1=ps[:, PR, 0:LG], op0=ALU.mult, op1=ALU.add).then_inc(lg_out, 1)
                    for n in (shares[t] if shares else ()):
                        late_step(n)

            def phase2(i, l0, l1):
                p = i - 1
                if l0:
                    dve.wait_ge(lg_out, TG * (i + 1))
                    gates(i + 1, gate0, lgs[:, :, ER0:LG], E0, SCALE0, gate0_step, dif0_ok, ex0_ok,
                          GATE_STEPS * i, None)
                    nc.vector.tensor_tensor(lw[:, :, :].rearrange("p t (e r) -> p t e r", r=R),
                                            lgs[:, :, 0:ER0].rearrange("p t (e r) -> p t e r", r=R),
                                            gate0["w"][:, :, :].unsqueeze(3).to_broadcast([P, TG, E0, R]),
                                            ALU.mult).then_inc(lw_ok, 1)
                if l1:
                    dve.wait_ge(pj_mm, i)
                    dve.wait_ge(pj_ctx_ok, i)
                    nc.vector.tensor_tensor(pj[:, :, :], ps[:, PR, 0:TG * PJ].rearrange("p (t e) -> p t e", e=PJ),
                                            pj_ctx[:, :, :], ALU.add).then_inc(pj_ok, 1)
                    dve.wait_ge(pj_ok, i)
                    gates(i, gate1, pj[:, :, ER1:PJ], E1, SCALE1, gate1_step, dif1_ok, ex1_ok,
                          GATE_STEPS * p, None)
                    nc.vector.tensor_tensor(mw[:, :, :].rearrange("p t (e r) -> p t e r", r=R),
                                            pj[:, :, 0:ER1].rearrange("p t (e r) -> p t e r", r=R),
                                            gate1["w"][:, :, :].unsqueeze(3).to_broadcast([P, TG, E1, R]),
                                            ALU.mult).then_inc(mw_ok, 1)
                if l0:
                    dve.wait_ge(lwT_hi, i + 1)
                    minus_hi(lwTl[:, :], ps[:, TP0, :], lwTh[:, :]).then_inc(lwT_lo, 1)
                    if not l1:
                        for n in (*range(N2, N2 + 2), "ctx", *range(N2 + 2, N1)):
                            late_step(n)

                def make_x1(t):
                    dve.wait_ge(y_mm, TG * i + t + 1)
                    dve.wait_ge(xb_ok, TG * i + t + 1)
                    if l1:
                        dve.wait_ge(x1p_ok, TG * p + t + 1)
                    nc.vector.tensor_tensor(x1[:, t, :], ps[:, y_bank[t], :], xb[:, t, :], ALU.add).then_inc(x1_ok, 1)

                def make_out(t):
                    bank = d_bank(t, l0)
                    dve.wait_ge(d_mm, TG * p + t + 1)
                    dve.wait_ge(x1p_ok, TG * p + t + 1)
                    dve.wait_ge(out_done[t], 16 * i)
                    if l0 or t:
                        nc.vector.tensor_tensor(outb[:, t, :], ps[:, bank, :], x1p[:, t, :], ALU.add).then_inc(out_ok, 1)
                    else:
                        for half, ready in ((slice(0, D // 2), half_ok), (slice(D // 2, D), out_ok)):
                            nc.vector.tensor_tensor(outb[:, t, half], ps[:, bank, half], x1p[:, t, half],
                                                    ALU.add).then_inc(ready, 1)

                if l0:
                    for t in range(TG - 1):
                        make_x1(t)
                if l1:
                    for a in range(2):
                        dve.wait_ge(mwT_hi, 2 * p + a + 1)
                        minus_hi(mw_half(mwT, 1, a), mw_half(ps, a, a), mw_half(mwT, 0, a)).then_inc(mwT_lo, 1)
                    make_out(0)
                    make_out(1)
                if l0:
                    dve.wait_ge(x1T_hi, TG * i + 1)
                    minus_hi(x1Tl[:, 0, :], ps[:, TP1, :], x1Th[:, 0, :]).then_inc(x1T_lo, 1)
                if l0:
                    make_x1(TG - 1)
                if l1:
                    make_out(2)
                    make_out(3)

            dve.sem_inc(out_ok, TG)
            phase1(0, True, False, shares)
            phase2(0, True, False)
            with nc.vector.Fori(1, G) as i:
                phase1(i, True, True)
                phase2(i, True, True)
            phase1(G, False, True)
            phase2(G, False, True)

        @block.tensor
        def _(pe):
            def prep(n):
                u = units[n]
                for s, v in u["need"]:
                    pe.wait_ge(s, v)
                if u["after"]:
                    pe.wait_ge(prep_ok, u["after"])
                transposes(u).then_inc(prep_mm, 1)

            def transposes(u):
                for col, src in u["moves"]:
                    rows, cols = src.shape
                    last = nc.tensor.transpose(ps[0:cols, u["bank"], col:col + rows], src, ident[0:rows, 0:rows])
                return last

            def keep_busy(bank, n):
                for _ in range(n):
                    nc.tensor.matmul(ps[:, bank, 0:2 * P], ones_r[:, :], ones_r[:, :].unsqueeze(1).to_broadcast([P, 2, P]), start=True, stop=True)

            pe.wait_ge(consts, 3)
            keep_busy(Y + 2, 5)
            pe.wait_ge(in_cond, 16)
            nc.tensor.transpose(ps[:, MISC, 0:NB], cond_s[:, :], ident[0:NB, 0:NB]).then_inc(condT_mm, 1)
            keep_busy(Y + 2, 3)
            pe.wait_ge(in_w0, 16)
            pe.wait_ge(condT_ok, 1)
            nc.tensor.matmul(ps[:, MISC, 0:NB], w0_s[:, :], condT[:, :], start=True, stop=True).then_inc(h1_mm, 1)
            keep_busy(Y + 2, 4)
            pe.wait_ge(in_w1, 16)
            pe.wait_ge(h1_ok, 1)
            nc.tensor.matmul(ps[:, MISC, 0:NB], w1_s[:, :], h1T[:, :], start=True, stop=True).then_inc(h2_mm, 1)
            keep_busy(Y + 2, 5)
            pe.wait_ge(consts, 2)
            pe.wait_ge(in_b2, 16)
            nc.tensor.matmul(ps[0:NB, Y, 0:K0], ones[0:1, 0:NB], b2_s[:, :], start=True, stop=False)
            pe.wait_ge(in_w2, 16)
            pe.wait_ge(h2_ok, 1)
            nc.tensor.matmul(ps[0:NB, Y, 0:K0], h2T[:, :], w2_s[:, :], start=False, stop=True).then_inc(att_mm, 1)
            keep_busy(Y + 2, 8)
            pe.wait_ge(att_ok, 1)
            nc.tensor.transpose(ps[0:96, MISC, 0:NB], att3[:, :, :].rearrange("b n k -> b (n k)"),
                                ident[0:NB, 0:NB]).then_inc(attT_mm, 1)
            pe.wait_ge(in_lg, 32)
            for u in lg_units:
                transposes(u).then_inc(lgT_mm, 1)
            keep_busy(Y + 2, 3)
            pe.wait_ge(mixw3_ok, 1)
            pe.wait_ge(mixw3_hi, 2)
            pe.wait_ge(att3_ok, 1)
            for m in range(C * C // P):
                last = nc.tensor.matmul(ps[:, PR, m * NB:(m + 1) * NB], mixw3[0:64 + K0, m * P:(m + 1) * P],
                                        att3T[0:64 + K0, :], start=True, stop=True)
            last.then_inc(mixw_mm, 1)
            pe.wait_ge(in_mixb, 16)
            pe.wait_ge(attT_ok, 1)
            nc.tensor.matmul(ps[:, MISC, 0:NB], mixb_s[:, :, :].rearrange("k j o -> k (j o)"), attT[:, :],
                             start=True, stop=True).then_inc(mixb_mm, 1)
            pe.wait_ge(lg_ok, 2)
            for n in range(FIRST):
                prep(n)
            pe.wait_ge(mixw_a, 1)
            pe.wait_ge(mixw_v, 1)

            def hi_lo(dst, stationary, moving, start=True, stop=True):
                n = len(stationary)
                for c in range(n):
                    (sh, sl), (mh, ml) = stationary[c], moving[c]
                    nc.tensor.matmul(dst, sh, mh, start=start and c == 0, stop=False)
                    end = stop and c == n - 1
                    last = nc.tensor.matmul(dst, sh, ml, start=False, stop=end and sl is None)
                    if sl is not None:
                        last = nc.tensor.matmul(dst, sl, mh, start=False, stop=end)
                return last

            def transpose_x1(t):
                for c in range(DC):
                    last = nc.tensor.transpose(ps[:, TP1, c * P:(c + 1) * P], x1[:, t, c * P:(c + 1) * P], ident[:, :])
                last.then_inc(x1T_mm, 1)

            def project_x1(t, bank, k0, k1):
                s = t % 2
                cols = [slice(c * P, (c + 1) * P) for c in range(DC)]
                return hi_lo(ps[:, bank, 0:(k1 - k0) * PJ],
                             [(x1Th[:, s, c], x1Tl[:, s, c]) for c in cols],
                             [(pj_h[:, c, k0:k1, :].rearrange("p k e -> p (k e)"),
                               pj_l[:, c, k0:k1, :].rearrange("p k e -> p (k e)")) for c in range(DC)])

            def base(t):
                cols = [slice(c * P, (c + 1) * P) for c in range(DC)]
                hi_lo(ps[:, y_bank[t], :], [(c0h[:, t, c], c0l[:, t, c]) for c in cols],
                      [(base_h[:, c, :], base_l[:, c, :]) for c in range(DC)], stop=False)

            def experts0(t):
                cols = slice(t * P, (t + 1) * P)
                hi_lo(ps[:, y_bank[t], :], [(lwTh[:, cols], lwTl[:, cols])], [(lb_h[:, :], lb_l[:, :])],
                      start=False).then_inc(y_mm, 1)

            def experts1(t, bank):
                cols = slice(t * P, (t + 1) * P)
                nc.tensor.matmul(ps[:, bank, :], mwT[:, cols], b1e_h[:, :], start=True, stop=False)
                nc.tensor.matmul(ps[:, bank, :], mwT[:, cols], b1e_l[:, :], start=False,
                                 stop=True).then_inc(d_mm, 1)

            def late_step(n):
                if n == "lg_sum":
                    pe.wait_ge(lgc_ok, 1)
                    pe.wait_ge(mixb_ok, 1)
                    nc.tensor.matmul(ps[:, MISC, 0:LG], ones[:, :], lg_c[:, :], start=True, stop=True).then_inc(sum_mm, 1)
                elif n == "pj_sum":
                    pe.wait_ge(pjc_ok, 1)
                    pe.wait_ge(sum_ok, 2)
                    nc.tensor.matmul(ps[:, MISC, 0:PJ], ones[:, :], pj_c[:, :], start=True, stop=True).then_inc(sum_mm, 1)
                elif n == "base_sum":
                    pe.wait_ge(diag_ok, 1)
                    pe.wait_ge(sum_ok, 1)
                    nc.tensor.matmul(ps[:, MISC, 0:D], ones[:, :], base_diag.rearrange("p o q -> p (o q)"),
                                     start=True, stop=True).then_inc(sum_mm, 1)
                elif n == "ctx":
                    pe.wait_ge(prep_ok, N2 - 1)
                    pe.wait_ge(lg_out, TG)
                    nc.tensor.matmul(ps[:, PR, 0:NB], ctxwT[:, :], condT[:, :], start=True, stop=True).then_inc(ctx_mm, 1)
                elif n not in ("base_rows", "pj_c") and n >= FIRST:
                    prep(n)

            def mix(i, t, first):
                pe.wait_ge(x_in[t], 16 * (i + 1))
                if first and t > 1:
                    pe.wait_ge(c0_hi, t - 1)
                elif not first and t:
                    pe.wait_ge(c0_hi, TG * i + t)
                for c in range(DC):
                    last = nc.tensor.matmul(ps[:, c0_bank(t, not first), c * P:(c + 1) * P], xr[:, t, c * P:(c + 1) * P],
                                            mixT[:, bass.ds(TG * i + t, 1), :].rearrange("p a o -> p (a o)"),
                                            start=True, stop=True)
                last.then_inc(c0_mm, 1)

            def phase1(i, l0, l1, shares=None):
                p = i - 1
                for t in range(TG):
                    if l0 and (t == 0 or not shares):
                        mix(i, t, shares)
                    for n in (shares[t] if shares else ()):
                        late_step(n)
                    if shares and t + 1 < TG:
                        mix(i, t + 1, shares)
                    if l1:
                        pe.wait_ge(x1T_lo, TG * p + t + 1)
                        if t + 1 < TG:
                            transpose_x1(t + 1)
                        za, zb = z_banks(t, l0)
                        if not l0 and t == 0:
                            pe.wait_ge(x1_ok, TG * i)
                        elif t <= (0 if l0 else 1):
                            pe.wait_ge(out_ok, TG * p + 3)
                        elif l0:
                            pe.wait_ge(za_lo, TG * p + t)
                        else:
                            pe.wait_ge(za_lo, TG * p + t - 1)
                        project_x1(t, za, 0, TA).then_inc(za_mm, 1)
                        if t <= (0 if l0 else 1):
                            if l0 or t:
                                pe.wait_ge(out_ok, TG * p + 4)
                        elif l0:
                            pe.wait_ge(zb_lo, TG * p + t)
                        else:
                            pe.wait_ge(zb_lo, TG * p + t - 1)
                        project_x1(t, zb, TA, TAPS).then_inc(zb_mm, 1)
                    if l0:
                        pe.wait_ge(c0_full, TG * i + t + 1)
                        if t:
                            pe.wait_ge(lg_out, TG * i + t)
                        elif shares:
                            pe.wait_ge(mixw_a, 2)
                            pe.wait_ge(mixw_v, 2)
                        for c in range(DC):
                            last = nc.tensor.matmul(ps[:, PR, 0:LG], c0f[:, t, c * P:(c + 1) * P], lgT[:, c, :],
                                                    start=c == 0, stop=c == DC - 1)
                        last.then_inc(lg_mm, 1)

            def phase2(i, l0, l1):
                p = i - 1
                if l0:
                    pe.wait_ge(c0_lo, TG * i + 1)
                    base(0)
                    if not l1:
                        pe.wait_ge(prep_ok, N2)
                if l1:
                    if l0:
                        pe.wait_ge(lg_out, TG * (i + 1))
                    for ready, taps in ((za_lo, range(TA)), (zb_lo, range(TA, TAPS))):
                        pe.wait_ge(ready, TG * i)
                        last = hi_lo(ps[:, PR, 0:TG * PJ], [(tap_h[:, k, :], tap_l[:, k, :]) for k in taps],
                                     [(zh[:, :, k, :], zl[:, :, k, :]) for k in taps],
                                     start=ready is za_lo, stop=ready is zb_lo)
                    last.then_inc(pj_mm, 1)
                    if not l0:
                        keep_busy(TP0, 28)
                if l0:
                    pe.wait_ge(c0_lo, TG * i + 2)
                    base(1)
                    if not l1:
                        late_step("base_sum")
                    pe.wait_ge(lw_ok, i + 1)
                    for t in range(TG):
                        last = nc.tensor.transpose(ps[:, TP0, t * P:(t + 1) * P], lw[:, t, :], ident[:, :])
                    last.then_inc(lwT_mm, 1)
                    if not l1:
                        pe.wait_ge(c0_hi, TG)
                        prep(N2)
                        prep(N2 + 1)
                    pe.wait_ge(c0_lo, TG * i + 3)
                    base(2)
                    if not l1:
                        late_step("pj_sum")
                        late_step("ctx")
                    if not l1:
                        prep(N2 + 2)
                        prep(N2 + 3)
                    pe.wait_ge(lwT_lo, i + 1)
                    for t in range(TG - 1):
                        experts0(t)
                if l1:
                    pe.wait_ge(mw_ok, i)
                    for q in range(TG // 2):
                        last = nc.tensor.transpose(ps[:, TP1, q * P:(q + 1) * P],
                                                   mw[:, 2 * q:2 * q + 2, :].rearrange("p a e -> p (a e)"), ident[:, :])
                    last.then_inc(mwT_mm, 1)
                    if not l0:
                        keep_busy(TP0, 10)
                if l0:
                    pe.wait_ge(c0_lo, TG * i + 4)
                    pe.wait_ge(x1_ok, TG * i + 1)
                    base(3)
                if l1:
                    for t in range(2):
                        pe.wait_ge(mwT_lo, 2 * p + t + 1)
                        experts1(t, d_bank(t, l0))
                if l0:
                    transpose_x1(0)
                    experts0(3)
                if l1:
                    for t in (2, 3):
                        if l0:
                            pe.wait_ge(out_ok, TG * i + t - 1)
                        experts1(t, d_bank(t, l0))

            phase1(0, True, False, shares)
            pe.wait_ge(prep_ok, N2 - 1)
            phase2(0, True, False)
            pe.wait_ge(prep_ok, N1)
            pe.wait_ge(ctx_ok, 1)
            pe.wait_ge(sum_ok, 3)
            pe.wait_ge(in_pj, 32)
            with nc.tensor.Fori(1, G) as i:
                phase1(i, True, True)
                phase2(i, True, True)
            phase1(G, False, True)
            phase2(G, False, True)


_INS = ["x", "cond_128", "fside_S_0", "L0_cond_W0", "L0_cond_b0", "L0_cond_W1", "L0_cond_b1", "L0_cond_W2",
        "L0_cond_b2", "L0_cond_weight", "L0_cond_bias_k", "L0_ffn_gate_w", "L0_ffn_base_w", "L0_ffn_base_b",
        "L0_ffn_lora_A", "L0_ffn_lora_B", "L1_cond_weight", "L1_cond_c_weight", "L1_ffn_router_w",
        "L1_ffn_A", "L1_ffn_B"]
_OUTS = [((64, 32, 512), "float32")]


def kernel(**inputs):
    import numpy as _np
    import concourse.bacc as _bacc
    from concourse import mybir as _mybir
    from concourse.bass_utils import run_bass_kernel_spmd as _run

    nc = _bacc.Bacc("TRN2", target_bir_lowering=False, num_devices=1)
    arrays, args = {}, []
    for name in _INS:
        a = _np.ascontiguousarray(inputs[name])
        arrays[f"in_{name}_dram"] = a
        args.append(nc.dram_tensor(f"in_{name}_dram", a.shape, _mybir.dt.from_np(a.dtype), kind="ExternalInput").ap())
    for i, (shape, dtype) in enumerate(_OUTS):
        dt = _mybir.dt.from_np(_np.dtype(dtype))
        args.append(nc.dram_tensor(f"out_{i}_dram", shape, dt, kind="ExternalOutput").ap())
    two_layer_mixer(nc, *args)
    r = _run(nc, [arrays], core_ids=[0])
    return r.results[0]["out_0_dram"]
```
